# Optimizing a Trainium2 kernel written in Bass

```python
import numpy as np
import jax
import jax.numpy as jnp

def _softmax(x, axis=-1):
    return jax.nn.softmax(x, axis=axis)

def _gelu(x):
    return jax.nn.gelu(x, approximate=True)

def _silu(x):
    return jax.nn.silu(x)

def _sigmoid(x):
    return jax.nn.sigmoid(x)

def _layernorm(x, axis=-1, eps=1e-05):
    m = jnp.mean(x, axis=axis, keepdims=True)
    v = jnp.var(x, axis=axis, keepdims=True)
    return (x - m) / jnp.sqrt(v + eps)

def _scatter_add(tgt, idx, src, axis=0):
    return tgt.at[idx].add(src)

def _segment_sum(src, seg, n):
    return jax.ops.segment_sum(src, seg, n)
kernel_name = 'mk_vit_tower_cls_d1_tok_img1024_r4_2d10aa'

def setup_inputs(seed: int=0):
    np.random.seed(seed)
    _w = jnp.asarray

    def _rec_inputs():
        import jax
        import jax.numpy as jnp
        _rk = jax.random.key(seed)
        x = -0.00150118 + 0.499729 * jax.random.normal(jax.random.fold_in(_rk, 1), (8, 256, 64, 2), jnp.float32)
        cls_tok = 0.02 * jax.random.normal(jax.random.fold_in(_rk, 5), (1, 1, 256), jnp.float32)
        return (x, cls_tok)
    x, cls_tok = _rec_inputs()

    def _L0_tok_setup():
        import jax, jax.numpy as jnp
        import numpy as np
        import math
        H = 256
        N = 64
        CH = 1
        SEQ_L = 256
        key = jax.random.key(seed)
        k1, k2, k3, k4 = jax.random.split(key, 4)
        log_dt = jax.random.uniform(k1, (H,), dtype=jnp.float32, minval=math.log(0.001), maxval=math.log(0.1))
        inv_A_real = jnp.log(0.5 * jnp.ones((H, N), jnp.float32)) + 0.1 * jax.random.normal(k2, (H, N), dtype=jnp.float32)
        A_imag = jnp.broadcast_to(math.pi * jnp.arange(N, dtype=jnp.float32), (H, N)).copy()
        B_ri = jax.random.normal(k3, (H, N, 2), dtype=jnp.float32) * 0.5
        C_ri = jax.random.normal(k4, (CH, H, N, 2), dtype=jnp.float32) * 0.5
        return {'log_dt': log_dt, 'inv_A_real': inv_A_real, 'A_imag': A_imag, 'B_ri': B_ri, 'C_ri': C_ri, 'L': SEQ_L}
    _L0_tok_all = _L0_tok_setup()
    _L0_tok_in = {k: v for k, v in _L0_tok_all.items() if k in ('log_dt', 'inv_A_real', 'A_imag', 'B_ri')}
    del _L0_tok_all

    def _L0_attn_setup():
        import jax, jax.numpy as jnp
        import numpy as np
        N_HEAD = 16
        EPS = 1e-06

        def _rotate_half(x):
            d = x.shape[-1] // 2
            return jnp.concatenate((-x[..., d:], x[..., :d]), axis=-1)

        def _rms_norm(x, w, eps=EPS):
            d = x.shape[-1]
            rms = jnp.linalg.norm(x, axis=-1, keepdims=True) * d ** (-0.5)
            return w * (x / (rms + eps))
        key = jax.random.key(seed)
        ks = jax.random.split(key, 3)
        B, T, C = (4, 512, 256)
        x = jax.random.normal(ks[0], (B, T, C), dtype=jnp.float32)
        W_kqv = jax.random.normal(ks[1], (3 * C, C), dtype=jnp.float32) * C ** (-0.5)
        W_proj = jax.random.normal(ks[2], (C, C), dtype=jnp.float32) * C ** (-0.5)
        D = C // N_HEAD
        q_norm_w = jnp.ones((D,), dtype=jnp.float32)
        k_norm_w = jnp.ones((D,), dtype=jnp.float32)
        return {'x': x, 'W_kqv': W_kqv, 'W_proj': W_proj, 'q_norm_w': q_norm_w, 'k_norm_w': k_norm_w}
    _L0_attn_all = _L0_attn_setup()
    _L0_attn_in = {k: v for k, v in _L0_attn_all.items() if k in ('W_kqv', 'W_proj', 'q_norm_w', 'k_norm_w')}
    del _L0_attn_all

    def _L0_ffn_setup():
        import jax, jax.numpy as jnp
        import numpy as np
        B, S, H, NH, E, F = (4, 256, 256, 16, 8, 1024)
        D = H // NH
        EPS = 1e-05

        def _layernorm(x, g, b):
            mu = jnp.mean(x, axis=-1, keepdims=True)
            var = jnp.var(x, axis=-1, keepdims=True)
            return (x - mu) * jax.lax.rsqrt(var + EPS) * g + b
        key = jax.random.key(seed)
        ks = jax.random.split(key, 16)
        s = 0.02
        return {'x': jax.random.normal(ks[0], (B, S, H), jnp.float32), 'ln1_g': jnp.ones((H,), jnp.float32), 'ln1_b': jnp.zeros((H,), jnp.float32), 'ln2_g': jnp.ones((H,), jnp.float32), 'ln2_b': jnp.zeros((H,), jnp.float32), 'wq': jax.random.normal(ks[1], (H, H), jnp.float32) * s, 'bq': jnp.zeros((H,), jnp.float32), 'wk': jax.random.normal(ks[2], (H, H), jnp.float32) * s, 'bk': jnp.zeros((H,), jnp.float32), 'wv': jax.random.normal(ks[3], (H, H), jnp.float32) * s, 'bv': jnp.zeros((H,), jnp.float32), 'wo': jax.random.normal(ks[4], (H, H), jnp.float32) * s, 'bo': jnp.zeros((H,), jnp.float32), 'gate_w': jax.random.normal(ks[5], (H, E), jnp.float32) * s, 'gate_b': jnp.zeros((E,), jnp.float32), 'w1': jax.random.normal(ks[6], (E, H, F), jnp.float32) * s, 'b1': jnp.zeros((E, F), jnp.float32), 'w2': jax.random.normal(ks[7], (E, F, H), jnp.float32) * s, 'b2': jnp.zeros((E, H), jnp.float32)}
    _L0_ffn_all = _L0_ffn_setup()
    _L0_ffn_in = {k: v for k, v in _L0_ffn_all.items() if k in ('ln1_g', 'ln1_b', 'ln2_g', 'ln2_b', 'wq', 'bq', 'wk', 'bk', 'wv', 'bv', 'wo', 'bo', 'gate_w', 'gate_b', 'w1', 'b1', 'w2', 'b2')}
    del _L0_ffn_all
    return {'x': x, 'cls_tok': cls_tok, 'L0_tok_log_dt': _L0_tok_in['log_dt'], 'L0_tok_inv_A_real': _L0_tok_in['inv_A_real'], 'L0_tok_A_imag': _L0_tok_in['A_imag'], 'L0_tok_B_ri': _L0_tok_in['B_ri'], 'L0_attn_W_kqv': _L0_attn_in['W_kqv'], 'L0_attn_W_proj': _L0_attn_in['W_proj'], 'L0_attn_q_norm_w': _L0_attn_in['q_norm_w'], 'L0_attn_k_norm_w': _L0_attn_in['k_norm_w'], 'L0_ffn_ln1_g': _L0_ffn_in['ln1_g'], 'L0_ffn_ln1_b': _L0_ffn_in['ln1_b'], 'L0_ffn_ln2_g': _L0_ffn_in['ln2_g'], 'L0_ffn_ln2_b': _L0_ffn_in['ln2_b'], 'L0_ffn_wq': _L0_ffn_in['wq'], 'L0_ffn_bq': _L0_ffn_in['bq'], 'L0_ffn_wk': _L0_ffn_in['wk'], 'L0_ffn_bk': _L0_ffn_in['bk'], 'L0_ffn_wv': _L0_ffn_in['wv'], 'L0_ffn_bv': _L0_ffn_in['bv'], 'L0_ffn_wo': _L0_ffn_in['wo'], 'L0_ffn_bo': _L0_ffn_in['bo'], 'L0_ffn_gate_w': _L0_ffn_in['gate_w'], 'L0_ffn_gate_b': _L0_ffn_in['gate_b'], 'L0_ffn_w1': _L0_ffn_in['w1'], 'L0_ffn_b1': _L0_ffn_in['b1'], 'L0_ffn_w2': _L0_ffn_in['w2'], 'L0_ffn_b2': _L0_ffn_in['b2']}

def reference(x, cls_tok, L0_tok_log_dt, L0_tok_inv_A_real, L0_tok_A_imag, L0_tok_B_ri, L0_attn_W_kqv, L0_attn_W_proj, L0_attn_q_norm_w, L0_attn_k_norm_w, L0_ffn_ln1_g, L0_ffn_ln1_b, L0_ffn_ln2_g, L0_ffn_ln2_b, L0_ffn_wq, L0_ffn_bq, L0_ffn_wk, L0_ffn_bk, L0_ffn_wv, L0_ffn_bv, L0_ffn_wo, L0_ffn_bo, L0_ffn_gate_w, L0_ffn_gate_b, L0_ffn_w1, L0_ffn_b1, L0_ffn_w2, L0_ffn_b2):
    import jax
    import jax.numpy as jnp

    def _L0_tok_ref(log_dt, inv_A_real, A_imag, B_ri, C_ri, L):
        import jax, jax.numpy as jnp
        import numpy as np
        import math
        H = 256
        N = 64
        CH = 1
        SEQ_L = 256
        dt = jnp.exp(log_dt)
        A = -jnp.exp(inv_A_real) + 1j * A_imag
        B = B_ri[..., 0] + 1j * B_ri[..., 1]
        C = C_ri[..., 0] + 1j * C_ri[..., 1]
        dtA = A * dt[:, None]
        dA = (1.0 + dtA / 2) / (1.0 - dtA / 2)
        C_term = C * B[None]
        log_dA = jnp.log(dA)
        V = jnp.exp(log_dA[:, :, None] * jnp.arange(L))
        K = 2.0 * jnp.einsum('chn,hnl->chl', C_term, V).real
        return K.astype(jnp.float32)

    def _L0_attn_ref(x, W_kqv, W_proj, q_norm_w, k_norm_w):
        import jax, jax.numpy as jnp
        import numpy as np
        N_HEAD = 16
        EPS = 1e-06

        def _rotate_half(x):
            d = x.shape[-1] // 2
            return jnp.concatenate((-x[..., d:], x[..., :d]), axis=-1)

        def _rms_norm(x, w, eps=EPS):
            d = x.shape[-1]
            rms = jnp.linalg.norm(x, axis=-1, keepdims=True) * d ** (-0.5)
            return w * (x / (rms + eps))
        B, T, C = x.shape
        H = N_HEAD
        D = C // H
        kqv = x @ W_kqv.T
        k, q, v = jnp.split(kqv, 3, axis=2)

        def to_heads(t):
            return t.reshape(B, T, H, D).transpose(0, 2, 1, 3)
        k, q, v = (to_heads(k), to_heads(q), to_heads(v))
        inv_freq = 1.0 / 10000.0 ** (jnp.arange(0, D, 2, dtype=jnp.float32) / D)
        t_pos = jnp.arange(T, dtype=jnp.float32)
        freqs = t_pos[:, None] * inv_freq[None, :]
        freqs = jnp.concatenate((freqs, freqs), axis=-1)
        cos = jnp.cos(freqs)[None, None]
        sin = jnp.sin(freqs)[None, None]
        q = q * cos + _rotate_half(q) * sin
        k = k * cos + _rotate_half(k) * sin
        q = _rms_norm(q, q_norm_w)
        k = _rms_norm(k, k_norm_w)
        scores = jnp.einsum('bhtd,bhsd->bhts', q, k) / jnp.sqrt(jnp.float32(D))
        causal = jnp.triu(jnp.ones((T, T), dtype=bool), k=1)
        scores = jnp.where(causal[None, None], -jnp.inf, scores)
        att = jax.nn.softmax(scores, axis=-1)
        y = jnp.einsum('bhts,bhsd->bhtd', att, v)
        y = y.transpose(0, 2, 1, 3).reshape(B, T, C)
        return y @ W_proj.T

    def _L0_ffn_ref(x, ln1_g, ln1_b, ln2_g, ln2_b, wq, bq, wk, bk, wv, bv, wo, bo, gate_w, gate_b, w1, b1, w2, b2):
        import jax, jax.numpy as jnp
        import numpy as np
        B, S, H, NH, E, F = (4, 256, 256, 16, 8, 1024)
        D = H // NH
        EPS = 1e-05

        def _layernorm(x, g, b):
            mu = jnp.mean(x, axis=-1, keepdims=True)
            var = jnp.var(x, axis=-1, keepdims=True)
            return (x - mu) * jax.lax.rsqrt(var + EPS) * g + b
        b, s, h = x.shape
        hn = _layernorm(x, ln1_g, ln1_b)
        q = (hn @ wq + bq).reshape(b, s, NH, D).transpose(0, 2, 1, 3)
        k = (hn @ wk + bk).reshape(b, s, NH, D).transpose(0, 2, 1, 3)
        v = (hn @ wv + bv).reshape(b, s, NH, D).transpose(0, 2, 1, 3)
        scores = jnp.einsum('bhqd,bhkd->bhqk', q, k) / jnp.sqrt(jnp.float32(D))
        attn = jax.nn.softmax(scores, axis=-1)
        o = jnp.einsum('bhqk,bhkd->bhqd', attn, v)
        o = o.transpose(0, 2, 1, 3).reshape(b, s, h)
        x = x + (o @ wo + bo)
        hn2 = _layernorm(x, ln2_g, ln2_b).reshape(-1, h)
        logits = hn2 @ gate_w + gate_b
        idx = jnp.argmax(logits, axis=-1)
        mid = jax.nn.relu(jnp.einsum('th,ehf->etf', hn2, w1) + b1[:, None, :])
        y = jnp.einsum('etf,efh->eth', mid, w2) + b2[:, None, :]
        moe = y[idx, jnp.arange(hn2.shape[0])]
        return x + moe.reshape(b, s, h)
    h = _L0_tok_ref(L0_tok_log_dt, L0_tok_inv_A_real, L0_tok_A_imag, L0_tok_B_ri, x, 256)
    h = jnp.concatenate([jnp.broadcast_to(cls_tok, (h.shape[0], 1, h.shape[2])), h], axis=1)
    h = h + _L0_attn_ref(_layernorm(h, axis=-1), L0_attn_W_kqv, L0_attn_W_proj, L0_attn_q_norm_w, L0_attn_k_norm_w)
    h = h + _L0_ffn_ref(_layernorm(h, axis=-1), L0_ffn_ln1_g, L0_ffn_ln1_b, L0_ffn_ln2_g, L0_ffn_ln2_b, L0_ffn_wq, L0_ffn_bq, L0_ffn_wk, L0_ffn_bk, L0_ffn_wv, L0_ffn_bv, L0_ffn_wo, L0_ffn_bo, L0_ffn_gate_w, L0_ffn_gate_b, L0_ffn_w1, L0_ffn_b1, L0_ffn_w2, L0_ffn_b2)
    return h

_drawn_inputs = setup_inputs


def setup_inputs(seed=0):
    import zlib

    import numpy as np

    out = dict(_drawn_inputs(seed))
    spreads = {'L0_attn_q_norm_w': (1.0, 0.6),
     'L0_attn_k_norm_w': (1.0, 0.6),
     'L0_ffn_ln1_g': (1.0, 0.6),
     'L0_ffn_ln1_b': (0.0, 0.8),
     'L0_ffn_ln2_g': (1.0, 0.6),
     'L0_ffn_ln2_b': (0.0, 0.586),
     'L0_ffn_bq': (0.0, 0.8),
     'L0_ffn_bk': (0.0, 2.0),
     'L0_ffn_bv': (0.0, 0.8),
     'L0_ffn_bo': (0.0, 0.344),
     'L0_ffn_gate_b': (0.0, 0.309),
     'L0_ffn_b1': (0.0, 0.8),
     'L0_ffn_b2': (0.0, 0.414)}
    factors = {'L0_ffn_wq': 8.0,
     'L0_ffn_wk': 8.0,
     'L0_ffn_wv': 8.0,
     'L0_ffn_wo': 5.971,
     'L0_ffn_w1': 2.805}
    for name, (base, spread) in spreads.items():
        noise = np.random.default_rng([zlib.crc32(name.encode()), seed]).standard_normal(out[name].shape)
        drawn = base * np.exp(spread * noise) if base else spread * noise
        out[name] = jnp.asarray(drawn.astype(out[name].dtype))
    for name, factor in factors.items():
        out[name] = (out[name] * factor).astype(out[name].dtype)
    return out
```

```python
from contextlib import ExitStack

import numpy as np

import concourse.bass as bass
from concourse import mybir

F32 = mybir.dt.float32
BF16 = mybir.dt.bfloat16
I32 = mybir.dt.int32
U32 = mybir.dt.uint32
ALU = mybir.AluOpType
ACT = mybir.ActivationFunctionType
AX = mybir.AxisListType.X

P = 128
B = 8
SEQ = 256
T = SEQ + 1
C = 256
HEADS = 16
D = C // HEADS
NS = 64
KC = C // P
TILES = 2 + B * SEQ // P
PARTS = 6
KS = PARTS * D
GROUPS = HEADS // 4
E = 8
F = 1024
FC = F // P
SLOT_TILES = 24
SLOTS = SLOT_TILES * P
ROW = 2 * C + 1
NEG = -1.0e30
NO_ROW = 1 << 20
AB, AA = 64, 4
CH = 4
EXP_MIN, EXP_MAX = -87.3, 88.7
ROUND = 1.5 * 2.0 ** 23
LN2_HIGH = 355.0 / 512
LN2_LOW = float(np.log(2)) - LN2_HIGH
HC = 32


def constants():
    p = np.arange(P)
    cols = {}
    cols["ident"] = np.eye(P)
    cols["before"] = (p[:, None] < p[None, :]) * 1.0
    cols["ones"] = np.ones((P, P))
    inv_freq = (1.0 / 10000.0 ** (np.arange(0, D, 2, dtype=np.float32) / np.float32(D))).astype(np.float32)
    pos = np.stack([np.zeros(P), 1 + p, 1 + P + p], 1).astype(np.float32)
    ang = (pos[:, :, None] * inv_freq).astype(np.float32)
    cos, sin = np.cos(ang), np.sin(ang)
    cols["cos"] = np.concatenate([cos, cos], -1).reshape(P, -1)
    cols["sin"] = np.concatenate([-sin, sin], -1).reshape(P, -1)
    h = np.arange(HEADS)
    own = np.zeros((P, HEADS, D))
    own[:HEADS] = (h[:, None] == h[None, :])[:, :, None]
    cols["own"] = own.reshape(P, -1)
    valid = np.ones((P, TILES))
    valid[B:, 0] = 0
    valid[:, 1] = 0
    cols["valid"] = valid
    cols["prefer"] = np.tile(E - np.arange(E), (P, TILES))
    cols["full"] = np.tile(P * np.arange(TILES - 1), (P, E))
    cols["tile_no"] = np.tile(np.repeat(np.arange(SLOT_TILES), E), (P, 1))
    restart = np.ones((P, E, TILES))
    restart[:, :, 0] = 0
    cols["restart"] = restart.reshape(P, -1)
    at, off = {}, 0
    for k, v in cols.items():
        at[k] = (off, v.shape[1])
        off += v.shape[1]
    table = np.concatenate(list(cols.values()), 1).astype(np.float32)
    halfs = {}
    halfs["identb"] = np.eye(P)
    halfs["mask_q"] = np.where(p[None, :] > p[:, None], NEG, 0.0)
    halfs["mask_k"] = np.where(p[:, None] > p[None, :], NEG, 0.0)
    selc = np.zeros((P, HEADS))
    for part in range(3):
        selc[32 * part + h, h] = 1
    halfs["selc"] = selc
    halfs["sel"] = np.repeat(selc[:, :, None], P, 2).reshape(P, -1)
    atb, off = {}, 0
    for k, v in halfs.items():
        atb[k] = (off, v.shape[1])
        off += v.shape[1]
    tableb = np.concatenate(list(halfs.values()), 1).astype(np.float32)
    out_row = np.full((P, TILES), NO_ROW)
    out_row[:B, 0] = np.arange(B) * T
    for b in range(B):
        for j in range(2):
            out_row[:, 2 + 2 * b + j] = b * T + 1 + j * P + p
    return table, at, tableb, atb, out_row.astype(np.int32)


def after(eng, semaphore, value):
    if not (isinstance(value, int) and value <= 0):
        eng.wait_ge(semaphore, value)


def col(x, n=1):
    return slice(x, x + n) if isinstance(x, int) else bass.ds(x, n)


def over(ap, axis, n):
    v = ap.unsqueeze(axis)
    shape = list(v.shape)
    shape[axis] = n
    return v.broadcast_to(shape)


class Layer:

    def __init__(self, name, causal):
        self.name, self.causal = name, causal
        self.s_front, self.s_out = (1, 5) if causal else (7, 1)
        self.s_norm = 1 if causal else 4
        self.s_square, self.s_high = (6, 11) if causal else (20, 10)


def bass_vit_tower(nc, A, out, at, atb, n_table, n_tableb):
    ctx = ExitStack()
    with ctx:
        def sb(name, shape, dt=F32, where=None):
            return (where or ctx).enter_context(nc.sbuf_tensor(name, shape, dt))

        def sem(name):
            return ctx.enter_context(nc.semaphore(name))

        psT = ctx.enter_context(nc.psum_tensor("psT", [P, 4, 512], F32))
        bank4 = ctx.enter_context(nc.psum_tensor("bank4", [P, 512], F32))
        bank5 = ctx.enter_context(nc.psum_tensor("bank5", [P, 512], F32))
        bank6 = ctx.enter_context(nc.psum_tensor("bank6", [P, 512], F32))
        bank7 = ctx.enter_context(nc.psum_tensor("bank7", [P, 512], F32))

        x_seq = nc.dram_tensor("x_seq", [B, SEQ, C], F32, kind="Internal").ap()
        v_cls = [nc.dram_tensor(f"v_cls{n}", [B, C], F32, kind="Internal").ap() for n in range(2)]
        x_sorted = nc.dram_tensor("x_sorted", [SLOTS, ROW], F32, kind="Internal").ap()

        rows = sb("rows", [P, TILES, ROW])
        rows_i = rows[:, :, :].bitcast(I32)
        table = sb("table", [P, n_table])
        w1a = sb("w1a", [P, E, F])
        gate_in = sb("gate_in", [P, KC, E])
        lnv = sb("lnv", [P, 3 * C + E])
        stat3 = sb("stat3", [P, 2, 6])
        mv3 = sb("mv3", [P, 2, 2])
        ve3 = sb("ve3", [P, 2, 1])
        rstd3 = sb("rstd3", [P, 2, 1])
        half = sb("half", [P, 2])

        def tab(name, parts=P):
            o, n = at[name]
            return table[0:parts, o:o + n]

        ident = tab("ident")

        tok = ExitStack()
        zin = sb("zin", [P, 5, P], F32, tok)
        cin = sb("cin", [P, 2, B, P], F32, tok)
        zp = sb("zp", [P, 2, 8, P], F32, tok)
        zn = sb("zn", [P, 6, P], F32, tok)
        hre = [sb(f"hre{n}", [P, HC, AB], F32, tok) for n in range(2)]
        him = [sb(f"him{n}", [P, HC, AB], F32, tok) for n in range(2)]
        gre = [sb(f"gre{n}", [P, HC, AA, B], F32, tok) for n in range(2)]
        gim = [sb(f"gim{n}", [P, HC, AA, B], F32, tok) for n in range(2)]
        t1 = sb("t1", [P, HC * 32], F32, tok)
        t2 = sb("t2", [P, HC * 32], F32, tok)
        t3 = [sb(f"t3{n}", [P, HC * 32], F32, tok) for n in range(2)]
        t4 = sb("t4", [P, HC * 32], F32, tok)
        xs_sb = sb("xs_sb", [P, 2, CH, 8, AB], F32, tok)
        zt = t1[:, :].rearrange("p (k r) -> p k r", k=8)
        pad = rows[:, 2, :]
        tok.close()

        att = ExitStack()
        tableb = sb("tableb", [P, n_tableb], BF16, att)

        def tabb(name, parts=P):
            o, n = atb[name]
            return tableb[0:parts, o:o + n]

        identb = tabb("identb")
        wqkv = sb("wqkv", [P, KC, 3 * C], F32, att)
        wout = sb("wout", [P, KC, C], F32, att)
        vecs = sb("vecs", [P, 3 * C + 2 * C], F32, att)
        QT = [sb(f"QT{n}", [KS, HEADS, T], BF16, att) for n in range(2)]
        KT = [sb(f"KT{n}", [KS, HEADS, T], BF16, att) for n in range(2)]
        QTc = sb("QTc", [KS, HEADS, B], BF16, att)
        KTc = sb("KTc", [KS, HEADS, B], BF16, att)
        QZ = sb("QZ", [KS, HEADS, 31], BF16, att)
        KZ = sb("KZ", [KS, HEADS, 31], BF16, att)
        VA = [sb(f"VA{n}", [P, 2, HEADS, 32], F32, att) for n in range(2)]
        VC = sb("VC", [HEADS, B, D], F32, att)
        VB = sb("VB", [P, HEADS, 32], F32, att)
        NM = sb("NM", [P, 2, HEADS], F32, att)
        NR = sb("NR", [P, 2, HEADS], F32, att)
        MS = sb("MS", [P, 2, 3, 32], BF16, att)
        NMC = sb("NMC", [HEADS, 1], F32, att)
        NRC = sb("NRC", [HEADS, 1], F32, att)
        MC = sb("MC", [HEADS, 1], BF16, att)
        M3 = [sb(f"M3{n}", [KS, T], BF16, att) for n in range(2)]
        EC = sb("EC", [P, T], F32, att)
        stat = sb("stat", [P, 2, 6], F32, att)
        mv = sb("mv", [P, 2, 2], F32, att)
        ve = sb("ve", [P, 2, 1], F32, att)
        rstd = sb("rstd", [P, 2, 1], F32, att)
        stat2 = sb("stat2", [P, 2, 6], F32, att)
        mv2 = sb("mv2", [P, 2, 2], F32, att)
        ve2 = sb("ve2", [P, 2, 1], F32, att)
        rstd2 = sb("rstd2", [P, 2, 1], F32, att)
        hn = sb("hn", [P, 2, C], F32, att)
        hnT = sb("hnT", [P, 4, P], F32, att)
        vt = sb("vt", [P, 2, C], F32, att)
        qk = sb("qk", [P, 2, 2 * C], F32, att)
        ya = sb("ya", [P, 2, 2 * C], F32, att)
        yb = sb("yb", [P, 2, 2 * C], F32, att)
        ss = sb("ss", [P, 64], F32, att)
        msq = sb("msq", [P, 64], F32, att)
        root0 = sb("root0", [P, 64], F32, att)
        tmp = sb("tmp", [P, 64], F32, att)
        KSt = sb("KSt", [P, 2, HEADS, PARTS, D], BF16, att)
        QSt = sb("QSt", [P, 2, HEADS, PARTS, D], BF16, att)
        NPT = 8
        PT = [sb(f"PT{n}", [P, 2, T], F32, att) for n in range(NPT)]
        OT = sb("OT", [P, GROUPS, T], F32, att)
        OTc = sb("OTc", [P, GROUPS, B], F32, att)
        RZ = sb("RZ", [P, HEADS], F32, att)
        ON = sb("ON", [P, 2, C], F32, att)
        ONT = sb("ONT", [P, 4, P], F32, att)
        att.close()

        moe = ctx
        w1b = sb("w1b", [P, E, F], F32, moe)
        w2 = sb("w2", [P, E, FC, C], F32, moe)
        b1t = sb("b1t", [P, E, FC], F32, moe)
        b2r = sb("b2r", [P, E, C], F32, moe)
        GP = 3
        gn = [sb(f"gn{n}", [P, 2, C], F32, moe) for n in range(GP)]
        gT = [sb(f"gT{n}", [P, 4, P], F32, moe) for n in range(GP)]
        lg = sb("lg", [P, TILES, E], F32, moe)
        lmax = sb("lmax", [P, TILES], F32, moe)
        lc = sb("lc", [P, TILES, E], F32, moe)
        oh = sb("oh", [P, TILES, E], F32, moe)
        tot = sb("tot", [P, E, TILES], F32, moe)
        cum = sb("cum", [P, E, TILES], F32, moe)
        nt = sb("nt", [P, E], F32, moe)
        big = sb("big", [P, E * (TILES - 1)], F32, moe)
        ct = sb("ct", [P, E], F32, moe)
        base = sb("base", [P, E], F32, moe)
        slotf = sb("slotf", [P, TILES], F32, moe)
        slot = sb("slot", [P, TILES], U32, moe)
        exf = sb("exf", [P, SLOT_TILES, E], F32, moe)
        exr = sb("exr", [P, SLOT_TILES], F32, moe)
        ex = sb("ex", [P, SLOT_TILES], I32, moe)
        XB = 4
        xst = [rows[:, n, :] for n in range(XB)]
        yo = [rows[:, 4 + n // 2, (n % 2) * C:(n % 2 + 1) * C] for n in range(XB)]
        midT = [rows[:, 6 + 2 * n:8 + 2 * n, 0:512].rearrange(
            "p t (k q) -> p t k q", q=P) for n in range(2)]
        w1s = [rows[:, 10 + 4 * n:14 + 4 * n, 0:512] for n in range(2)]
        xT = [sb(f"xT{n}", [P, KC, P], F32, moe) for n in range(2)]

        in_tab = sem("in_tab"); in_z = sem("in_z"); in_cls = sem("in_cls")
        in_ln = sem("in_ln"); in_w1 = sem("in_w1"); in_w2 = sem("in_w2"); in_moe = sem("in_moe"); in_tabb = sem("in_tabb")
        filled = sem("filled"); pad_stored = sem("pad_stored")
        z_step = sem("z_step")
        h_one = sem("h_one")
        dve_step = sem("dve_step"); pool_step = sem("pool_step")
        x_ps = sem("x_ps"); x_sb = sem("x_sb"); x_stored = [sem(f"x_stored{n}") for n in range(2)]; x_loaded = sem("x_loaded")
        cleared = sem("cleared"); z_done = sem("z_done"); zi_done = sem("zi_done")

        layers = []
        for name, causal in (("a", True), ("b", False)):
            L = Layer(name, causal)
            L.in_w = sem(name + "_in_w"); L.in_vec = sem(name + "_in_vec"); L.stat = sem(name + "_stat")
            L.mv = sem(name + "_mv"); L.rstd = sem(name + "_rstd"); L.hn = sem(name + "_hn")
            L.hnT_ps = sem(name + "_hnT_ps"); L.hnT = sem(name + "_hnT"); L.kq_ps = sem(name + "_kq_ps")
            L.qk = sem(name + "_qk"); L.v_ps = sem(name + "_v_ps"); L.v = sem(name + "_v"); L.va = sem(name + "_va")
            L.parts = sem(name + "_parts"); L.rest = sem(name + "_rest")
            L.kt_ps = sem(name + "_kt_ps"); L.qt_ps = sem(name + "_qt_ps"); L.kt = sem(name + "_kt")
            L.qt = sem(name + "_qt"); L.cls = sem(name + "_cls"); L.col0 = sem(name + "_col0")
            L.sq_ps = sem(name + "_sq_ps")
            L.mx = sem(name + "_mx"); L.ms = sem(name + "_ms"); L.scq_ps = sem(name + "_scq_ps")
            L.mc = sem(name + "_mc"); L.m3_ps = sem(name + "_m3_ps"); L.m3 = sem(name + "_m3")
            L.sck_ps = sem(name + "_sck_ps"); L.ec = sem(name + "_ec"); L.vb = sem(name + "_vb")
            L.st_ps = sem(name + "_st_ps"); L.exp = sem(name + "_exp"); L.pv = sem(name + "_pv")
            L.ot_raw = sem(name + "_ot_raw"); L.to_ps = sem(name + "_to_ps"); L.on = sem(name + "_on")
            L.onT_ps = sem(name + "_onT_ps"); L.onT = sem(name + "_onT"); L.otc = sem(name + "_otc")
            L.pj_ps = sem(name + "_pj_ps"); L.h = sem(name + "_h"); L.v_out = sem(name + "_v_out")
            L.vc = sem(name + "_vc")
            if causal:
                L.rc = sem(name + "_rc"); L.turn = sem(name + "_turn"); L.root = sem(name + "_root")
            else:
                L.ck_ps = sem(name + "_ck_ps"); L.ck = sem(name + "_ck")
                L.stat_a = sem(name + "_stat_a"); L.mv_a = sem(name + "_mv_a"); L.rstd_a = sem(name + "_rstd_a")
                L.x2 = sem(name + "_x2"); L.hb = sem(name + "_hb")
            layers.append(L)

        r_stat = sem("r_stat"); r_mv = sem("r_mv"); r_rstd = sem("r_rstd")
        r_res = sem("r_res"); r_hn = sem("r_hn"); r_hb = sem("r_hb"); r_gn = sem("r_gn")
        r_gT_ps = sem("r_gT_ps"); r_gT = sem("r_gT"); r_lg_ps = sem("r_lg_ps"); r_lg = sem("r_lg")
        r_step = sem("r_step"); r_cnt_ps = sem("r_cnt_ps"); r_slot = sem("r_slot")
        r_ex = sem("r_ex"); sorted_out = sem("sorted_out")
        m_x = [sem(f"m_x{n}") for n in range(XB)]
        m_xT_ps = sem("m_xT_ps"); m_xT = sem("m_xT"); m_w = sem("m_w")
        m_midT_ps = sem("m_midT_ps"); m_midT = sem("m_midT"); m_y_ps = sem("m_y_ps"); m_yb = sem("m_yb")
        m_yo = sem("m_yo")
        m_out = [sem(f"m_out{n}") for n in range(XB)]

        passed = sem("passed")

        def settle(eng):
            eng.sem_inc(passed, 1)

        def store_rows(eng, n):
            eng.wait_ge(x_sb, 2 * CH - 1 + n)
            for j in range(4):
                for a in range(AA):
                    lane = 32 * j + B * a
                    eng.dma_start(
                        x_seq[:, n * P + 32 * j:n * P + 32 * (j + 1), a * AB:(a + 1) * AB],
                        xs_sb[lane:lane + B, n, :, :, :].rearrange("c q g b -> c (q g) b"),
                    ).then_inc(x_stored[n], 16)

        def load_rows(eng, n):
            eng.wait_ge(x_stored[n], 16 * 4 * AA)
            eng.dma_start(rows[:, 2:TILES, C:2 * C].rearrange("p (c j) f -> p c j f", j=2)[:, :, n, :],
                          x_seq[:, n * P:(n + 1) * P, :].rearrange("c p f -> p c f")).then_inc(x_loaded, 16)

        block = ctx.enter_context(nc.Block())

        @block.sync
        def _(sp):
            sp.dma_start(zin[:, :, :], A["z_in"]).then_inc(in_z, 16)
            sp.dma_start(cin[:, :, :, :], A["c_in"]).then_inc(in_z, 16)
            sp.dma_start(table[:, :], A["table"]).then_inc(in_tab, 16)
            sp.wait_ge(filled, 3)
            for n in range(SLOT_TILES):
                sp.dma_start(x_sorted[n * P:(n + 1) * P, :], pad).then_inc(pad_stored, 16)
            sp.wait_ge(pad_stored, 16 * SLOT_TILES)
            sp.dma_start(rows_i[:, :, 2 * C:ROW], A["out_row"].unsqueeze(2), allow_slow_non_contiguous=True).then_inc(in_cls, 16)
            sp.dma_start(rows[0:B, 0, C:2 * C], A["cls"]).then_inc(in_cls, 16)
            sp.dma_start(lnv[:, :], A["lnv"]).then_inc(in_ln, 16)
            sp.dma_start(gate_in[:, :, :], A["gate_w"].rearrange("(k p) e -> p k e", p=P)).then_inc(in_ln, 16)
            for e in range(E):
                sp.dma_start(w1a[:, e, :], A["w1"][e, 0:P, :]).then_inc(in_w1, 16)
            sp.wait_ge(z_done, CH)
            sp.wait_ge(zi_done, CH)
            sp.dma_start(tableb[:, :], A["tableb"]).then_inc(in_tabb, 16)
            for n, L in enumerate(layers):
                if n:
                    sp.wait_ge(layers[0].h, B + 1)
                sp.dma_start(wqkv[:, :, :], A["wqkv"][n].rearrange("(k p) f -> p k f", p=P)).then_inc(L.in_w, 16)
                sp.dma_start(wout[:, :, :], A["wout"][n].rearrange("(k p) f -> p k f", p=P)).then_inc(L.in_w, 16)
                sp.dma_start(vecs[:, :], A["vecs"][n]).then_inc(L.in_vec, 16)
                if n == 0:
                    store_rows(sp, 0)
                    load_rows(sp, 0)
                sp.wait_ge(L.v, 1)
                sp.dma_start(v_cls[n].rearrange("b (h d) -> b h d", d=D), vt[0:B, 0, :].rearrange("p (h d) -> p h d", d=D)).then_inc(L.v_out, 16)
                sp.wait_ge(L.v_out, 16)
                sp.dma_start(VC[:, :, :], v_cls[n].rearrange("b (h d) -> h b d", d=D)).then_inc(L.vc, 16)
            L = layers[1]
            sp.wait_ge(L.h, B + 1)
            sp.wait_ge(L.otc, B)
            sp.dma_start(b1t[:, :, :], A["b1t"]).then_inc(in_moe, 16)
            sp.dma_start(b2r[:, :, :], A["b2r"]).then_inc(in_moe, 16)
            for e in range(E):
                sp.dma_start(w1b[:, e, :], A["w1"][e, P:C, :]).then_inc(in_w1, 16)
            for e in range(E):
                sp.dma_start(w2[:, e, :, :], A["w2"][e].rearrange("(k p) f -> p k f", p=P)).then_inc(in_w2, 16)
            sp.wait_ge(sorted_out, 16 * (TILES - 1))
            for n in range(XB):
                sp.dma_start(xst[n], x_sorted[n * P:(n + 1) * P, :]).then_inc(m_x[n], 16)
            with sp.Fori(1, SLOT_TILES // XB) as m:
                for n in range(XB):
                    sp.wait_ge(m_out[n], 16 * m)
                    sp.dma_start(xst[n], x_sorted[bass.ds((XB * m + n) * P, P), :]).then_inc(m_x[n], 16)

        def bank(n):
            return {4: bank4, 5: bank5, 6: bank6, 7: bank7}[n]

        def tile_x(c, j):
            return rows[:, col(2 * c + j), C:2 * C].rearrange("p o f -> p (o f)")

        def tile_n(c, j):
            return rows[:, col(2 * c + j), 0:C].rearrange("p o f -> p (o f)")

        def q_from(L, i):
            return 1 + i * P if L.causal else 0

        def score_ps(L, h, j):
            if L.causal:
                return bank(5 + h % 2)[:, j * (1 + P):j * (1 + P) + 1 + (j + 1) * P]
            return bank(5 + h % 2)[:, j * SEQ:(j + 1) * SEQ]

        def score_t_ps(L, h, i):
            if L.causal:
                return psT[:, h % 4, i * SEQ:i * SEQ + SEQ - i * P]
            return psT[:, 2 * (h % 2) + i, 0:T]

        def weights(L, h, i):
            if L.causal:
                return PT[h % NPT][:, :, :].rearrange("p i q -> p (i q)")[:, i * SEQ:i * SEQ + SEQ - i * P]
            return PT[h % NPT][:, i, 0:T]

        def expert_tiles(eng, one):
            for n in range(XB):
                one(eng, 0, n)
            with eng.Fori(1, SLOT_TILES // XB - 1) as m:
                for n in range(XB):
                    one(eng, m, n)
            for n in range(XB):
                one(eng, SLOT_TILES // XB - 1, n)

        def expert_of(eng, s):
            return eng.value_load(ex[0:1, col(s)], min_val=0, max_val=E - 1)

        def pe_turn_tokens(pe, L, c):
            pe.wait_ge(L.hn if L.causal else L.hb, 2 * c + 2)
            for j in range(2):
                for k in range(KC):
                    mm = pe.transpose(bank7[:, (2 * j + k) * P:(2 * j + k + 1) * P], hn[:, j, k * P:(k + 1) * P], ident)
            mm.then_inc(L.hnT_ps, 1)

        def pe_keys_queries(pe, L, c, j):
            if j == 0:
                pe.wait_ge(L.hnT, c + 1)
            else:
                pe.wait_ge(L.qk, 2 * c + 1)
            for k in range(KC):
                mm = pe.matmul(bank7[:, :], hnT[:, 2 * j + k, :], wqkv[:, k, 0:2 * C], start=(k == 0), stop=(k == KC - 1))
            mm.then_inc(L.kq_ps, 1)

        def pe_v(pe, L, c):
            for j in range(2):
                for k in range(KC):
                    mm = pe.matmul(bank7[:, j * C:(j + 1) * C], hnT[:, 2 * j + k, :], wqkv[:, k, 2 * C:3 * C],
                                   start=(k == 0), stop=(k == KC - 1), skip_group_check=True)
            mm.then_inc(L.v_ps, 1)

        def pe_stacks(pe, L, c, steps=range(4)):
            for s in steps:
                j, h0 = s // 2, 8 * (s % 2)
                for q, (st, ps, out_sem, used) in enumerate(((KSt, bank5, L.kt_ps, L.kt), (QSt, bank6, L.qt_ps, L.qt))):
                    if s == 0:
                        pe.wait_ge(L.rest, 8 * c + 6 + 2 * q)
                        after(pe, used, 4 * c)
                    else:
                        pe.wait_ge(used, 4 * c + s)
                    pv = ps[:, :].bitcast(BF16)
                    for n in range(8):
                        mm = pe.transpose(pv[0:KS, n * P:(n + 1) * P],
                                          st[:, j, h0 + n, :, :].rearrange("p a d -> p (a d)"), identb)
                    mm.then_inc(out_sem, 1)

        def pe_scores(pe, L, c, buf, h):
            if h == 0:
                pe.wait_ge(L.kt, 4 * c + 4)
                pe.wait_ge(L.qt, 4 * c + 4)
                pe.wait_ge(L.col0, 3 * c)
            for j in range(2):
                if h >= 2 and j == 0:
                    pe.wait_ge(L.mx, 32 * (c - 1) + 2 * (h - 1))
                keys = slice(0, 1 + (j + 1) * P) if L.causal else slice(1, T)
                ps = score_ps(L, h, j)
                mm = pe.matmul(ps, QT[buf][:, h, 1 + j * P:1 + (j + 1) * P], KT[buf][:, h, keys],
                               start=True, stop=not L.causal, skip_group_check=True)
                if L.causal:
                    mm = pe.matmul(ps[:, 1 + j * P:1 + (j + 1) * P], identb, tabb("mask_q"),
                                   start=False, stop=True, skip_group_check=True)
                mm.then_inc(L.sq_ps, 1)

        def pe_class_scores(pe, L, c, buf):
            if not L.causal:
                for j in range(2):
                    for h in range(HEADS):
                        mm = pe.matmul(bank7[:, j * HEADS + h:j * HEADS + h + 1], QT[buf][:, h, 1 + j * P:1 + (j + 1) * P],
                                       KT[buf][:, h, 0:1], start=True, stop=True, skip_group_check=True)
                mm.then_inc(L.ck_ps, 1)

        def pe_class_queries(pe, L, c, buf):
            pe.wait_ge(L.mx, 32 * c)
            n = 1 if L.causal else T
            for h in range(HEADS):
                mm = pe.matmul(bank5[0:HEADS, 0:n], QZ[:, h, HEADS - 1 - h:2 * HEADS - 1 - h], KT[buf][:, h, 0:n],
                               start=(h == 0), stop=(h == HEADS - 1))
            mm.then_inc(L.scq_ps, 1)

        def pe_turn_maxima(pe, L, c):
            pe.wait_ge(L.ms, 4 * c)
            pv = bank6[:, :].bitcast(BF16)
            for j in range(2):
                mm = pe.transpose(pv[0:KS, j * P:(j + 1) * P], MS[:, j, :, :].rearrange("p a h -> p (a h)"), identb)
            mm.then_inc(L.m3_ps, 1)

        def pe_class_keys(pe, L, c, buf):
            pe.wait_ge(L.m3, c)
            pe.wait_ge(L.mc, 6 * c)
            pe.wait_ge(L.vb, 2 * c - 1)
            for h in range(HEADS):
                pe.matmul(bank7[0:HEADS, 0:T], KZ[:, h, HEADS - 1 - h:2 * HEADS - 1 - h], QT[buf][:, h, :],
                          start=(h == 0), stop=False)
            pe.matmul(bank7[0:HEADS, 0:T], tabb("selc", KS), M3[buf][:, :], start=False, stop=True).then_inc(L.sck_ps, 1)

        def pe_scores_t(pe, L, c, buf, h):
            n = HEADS * (c - 1) + h
            after(pe, L.exp, n - 3 if L.causal else n - 1)
            for i in range(2):
                ps = score_t_ps(L, h, i)
                q0 = q_from(L, i)
                pe.matmul(ps, KT[buf][:, h, 1 + i * P:1 + (i + 1) * P], QT[buf][:, h, q0:T],
                          start=True, stop=False, skip_group_check=True)
                if L.causal:
                    pe.matmul(ps[:, 0:P], identb, tabb("mask_k"),
                              start=False, stop=False, skip_group_check=True)
                mm = pe.matmul(ps, tabb("sel", KS)[:, h * P:(h + 1) * P], M3[buf][:, q0:T],
                               start=False, stop=True, skip_group_check=True)
            mm.then_inc(L.st_ps, 1)

        def pe_values(pe, L, c, buf, g):
            if g == 0:
                pe.wait_ge(L.ec, c)
                pe.wait_ge(L.va, c + 1)
                pe.wait_ge(L.vb, 2 * c)
            after(pe, L.ot_raw, GROUPS * (c - 1) + g)
            pe.matmul(bank4[:, 0:T], VB[:, 4 * g:4 * g + 4, :].rearrange("p h d -> p (h d)"), EC[:, :],
                      start=True, stop=False, skip_group_check=True)
            pe.wait_ge(L.exp, HEADS * (c - 1) + 4 * g + 4)
            for i in range(2):
                q0 = q_from(L, i)
                for k in range(4):
                    h = 4 * g + k
                    mm = pe.matmul(bank4[32 * k:32 * k + 32, q0:T], VA[buf][:, i, h, :], weights(L, h, i),
                                   start=False, stop=(i == 1), skip_group_check=True)
            mm.then_inc(L.pv, 1)

        def pe_turn_out(pe, L, c, j):
            if j == 0:
                pe.wait_ge(L.ot_raw, GROUPS * c)
            else:
                pe.wait_ge(L.on, 4 * (c - 1) + 2)
            for g in range(GROUPS):
                mm = pe.transpose(bank7[:, g * P:(g + 1) * P], OT[:, g, 1 + j * P:1 + (j + 1) * P], ident)
            mm.then_inc(L.to_ps, 1)

        def pe_turn_on(pe, L, c):
            pe.wait_ge(L.on, 4 * c)
            for j in range(2):
                for k in range(KC):
                    mm = pe.transpose(bank7[:, (2 * j + k) * P:(2 * j + k + 1) * P], ON[:, j, k * P:(k + 1) * P], ident)
            mm.then_inc(L.onT_ps, 1)

        def pe_project(pe, L, c):
            pe.wait_ge(L.onT, c)
            for j in range(2):
                for k in range(KC):
                    mm = pe.matmul(bank7[:, j * C:(j + 1) * C], ONT[:, 2 * j + k, :], wout[:, k, :],
                                   start=(k == 0), stop=(k == KC - 1), skip_group_check=True)
            mm.then_inc(L.pj_ps, 1)

        def pe_front(pe, L, c):
            after(pe, L.v, c)
            pe_turn_tokens(pe, L, c)
            pe_keys_queries(pe, L, c, 0)
            pe_keys_queries(pe, L, c, 1)
            pe.wait_ge(L.qk, 2 * c + 2)
            pe_v(pe, L, c)
            if c == 0:
                pe_stacks(pe, L, c)

        def pe_round(pe, L, k, buf, value=True, score=True, front=True, back=True):
            if value:
                pe.wait_ge(L.v, min(k + 2, B + 1) if isinstance(k, int) else k + 2)
                if not L.causal:
                    pe.wait_ge(L.ck, k)
                if back:
                    after(pe, L.h, k - 2)
                pe_class_keys(pe, L, k, buf)
            for h in range(HEADS):
                if value:
                    pe_scores_t(pe, L, k, buf, h)
                if score and h < 4:
                    pe_stacks(pe, L, k + 1, [h])
                if score:
                    for hh in score_heads(h):
                        pe_scores(pe, L, k + 1, 1 - buf, hh)
                if value and h % 4 == 1 and h >= 5:
                    pe_values(pe, L, k, buf, (h - 5) // 4)
                if front and h == L.s_front:
                    if back and L.s_out < L.s_front:
                        pe.wait_ge(L.h, k - 1)
                    elif value:
                        pe.wait_ge(L.ec, k)
                    else:
                        pe.wait_ge(L.v, k + 2)
                    pe_turn_tokens(pe, L, k + 2)
                if front and h in (L.s_front + 1, L.s_front + 2):
                    pe_keys_queries(pe, L, k + 2, h - L.s_front - 1)
                if front and h == L.s_front + 3:
                    pe.wait_ge(L.qk, 2 * (k + 2) + 2)
                    pe_v(pe, L, k + 2)
                if back and h == L.s_out:
                    if front and L.s_front < L.s_out:
                        pe.wait_ge(L.v, k + 3)
                    elif value:
                        pe.wait_ge(L.ec, k)
                    else:
                        pe.wait_ge(L.h, k - 2)
                    pe_turn_out(pe, L, k - 1, 0)
                if back and h == L.s_out + 1:
                    pe_turn_out(pe, L, k - 1, 1)
                if back and h == L.s_out + 3:
                    pe_turn_on(pe, L, k - 1)
                if back and h == L.s_out + 5:
                    pe_project(pe, L, k - 1)
                if score and h == 12 and not L.causal:
                    if front:
                        pe.wait_ge(L.v, k + 3)
                    elif back:
                        pe.wait_ge(L.h, k - 1)
                    pe_class_scores(pe, L, k + 1, 1 - buf)
                if score and h == 14:
                    pe_class_queries(pe, L, k + 1, 1 - buf)
                if score and h == 15:
                    pe_turn_maxima(pe, L, k + 1)
            if value:
                pe_values(pe, L, k, buf, 3)

        def score_heads(h):
            return range(max(h - 4, 0) * 8 // 5 if h < 14 else HEADS, min(max(h - 3, 0) * 8 // 5, HEADS))

        def rounds(eng, L, one):
            one(eng, L, 0, 0, value=False, back=False)
            one(eng, L, 1, 1, back=False)
            with eng.Fori(0, 2) as m:
                one(eng, L, 2 * m + 2, 0)
                one(eng, L, 2 * m + 3, 1)
            one(eng, L, 6, 0)
            one(eng, L, 7, 1, front=False)
            one(eng, L, 8, 0, front=False, score=False)
            one(eng, L, 9, 1, front=False, score=False, value=False)

        def pe_attention(pe, L):
            pe.wait_ge(L.in_w, 32)
            pe.wait_ge(in_tabb, 16)
            pe.wait_ge(cleared, 9)
            for c in range(2):
                pe_front(pe, L, c)
            rounds(pe, L, pe_round)
            pe.wait_ge(L.otc, B)
            pe.wait_ge(L.h, B)
            for g in range(GROUPS):
                mm = pe.transpose(bank7[0:B, g * P:(g + 1) * P], OTc[:, g, :], ident)
            mm.then_inc(L.to_ps, 1)
            pe.wait_ge(L.on, 4 * B + 2)
            for k in range(KC):
                mm = pe.transpose(bank7[:, k * B:(k + 1) * B], ON[0:B, 0, k * P:(k + 1) * P], ident[0:B, 0:B])
            mm.then_inc(L.onT_ps, 1)
            pe.wait_ge(L.onT, B + 1)
            for k in range(KC):
                mm = pe.matmul(bank7[0:B, 0:C], ONT[:, k, 0:B], wout[:, k, :], start=(k == 0), stop=(k == KC - 1))
            mm.then_inc(L.pj_ps, 1)

        def pe_routing(pe):
            pe.wait_ge(in_ln, 32)
            with pe.Fori(0, TILES // 2 // GP) as m:
                for n in range(GP):
                    pe.wait_ge(r_gn, GP * m + n + 1)
                    for j in range(2):
                        for k in range(KC):
                            mm = pe.transpose(bank(5 + n)[:, (2 * j + k) * P:(2 * j + k + 1) * P],
                                              gn[n][:, j, k * P:(k + 1) * P], ident)
                    mm.then_inc(r_gT_ps, 1)
                for n in range(GP):
                    pe.wait_ge(r_gT, GP * m + n + 1)
                    for j in range(2):
                        for k in range(KC):
                            mm = pe.matmul(psT[:, n, j * E:(j + 1) * E], gT[n][:, 2 * j + k, :], gate_in[:, k, :],
                                           start=(k == 0), stop=(k == KC - 1), skip_group_check=True)
                    mm.then_inc(r_lg_ps, 1)
                pe.wait_ge(r_lg, GP * m + GP)
            pe.wait_ge(r_step, 7)
            flat = oh[:, :, :].rearrange("p t e -> p (t e)")
            pe.matmul(bank5[:, 0:TILES * E], tab("before"), flat, start=True, stop=True)
            pe.matmul(bank6[:, 0:TILES * E], tab("ones"), flat, start=True, stop=True).then_inc(r_cnt_ps, 1)

        def pe_sorted_turn(pe, m, n):
            pe.wait_ge(m_x[n], 16 * m + 16)
            for k in range(KC):
                mm = pe.transpose(bank(5 + n % 2)[:, k * P:(k + 1) * P], xst[n][:, k * P:(k + 1) * P], ident)
            mm.then_inc(m_xT_ps, 1)

        def pe_hidden(pe, s, n):
            pe.wait_ge(m_w, 2 * s + 2)
            pe.wait_ge(m_xT, s + 1)
            after(pe, m_midT, FC * (s - 1))
            for f in range(FC):
                for k in range(KC):
                    mm = pe.matmul(psT[:, 2 * (n % 2) + f // 4, (f % 4) * P:(f % 4 + 1) * P],
                                   w1s[n % 2][:, 2 * k + f // 4, (f % 4) * P:(f % 4 + 1) * P],
                                   xT[n % 2][:, k, :], start=(k == 0), stop=(k == KC - 1), skip_group_check=True)
                if f % 4 == 3:
                    mm.then_inc(m_midT_ps, 1)

        def pe_result(pe, s, n):
            e = expert_of(pe, s)
            after(pe, m_yb, s - 1)
            for k in range(FC):
                pe.wait_ge(m_midT, FC * s + k + 1)
                mm = pe.matmul(bank(4 + 3 * (n % 2))[:, 0:C], midT[n % 2][:, k // 4, k % 4, :],
                               w2[:, bass.ds(e, 1), k, :].rearrange("p o f -> p (o f)"),
                               start=(k == 0), stop=(k == FC - 1))
            mm.then_inc(m_y_ps, 1)

        def pe_expert_tile(pe, m, n):
            s = XB * m + n
            if not (isinstance(s, int) and s == SLOT_TILES - 1):
                pe_sorted_turn(pe, m + (n + 1) // XB, (n + 1) % XB)
            pe_hidden(pe, s, n)
            if not (isinstance(s, int) and s == 0):
                pe_result(pe, s - 1, (n - 1) % XB)

        def pe_experts(pe):
            pe.wait_ge(r_ex, 1)
            pe.wait_ge(r_slot, 1)
            pe.wait_ge(in_w1, 32 * E)
            pe.wait_ge(in_w2, 16 * E)
            pe_sorted_turn(pe, 0, 0)
            expert_tiles(pe, pe_expert_tile)
            pe_result(pe, SLOT_TILES - 1, XB - 1)

        def heads_of(y, kq):
            return y[:, :, kq * C:(kq + 1) * C].rearrange("p j (h d) -> p j h d", d=D)

        def act_tokens(act, L, c):
            act.wait_ge(L.hnT_ps, c + 1)
            act.activation(hnT[:, :, :].rearrange("p k q -> p (k q)"), bank7[:, :], ACT.Copy).then_inc(L.hnT, 1)

        def act_keys_queries(act, L, c, j):
            if L.causal:
                act.wait_ge(L.kq_ps, 2 * c + j + 1)
                if j == 0:
                    after(act, L.turn, 14 * c)
                act.activation(qk[:, j, :], bank7[:, :], ACT.Copy).then_inc(L.qk, 1)

        def act_v(act, L, c):
            if L.causal:
                act.wait_ge(L.v_ps, c + 1)
                after(act, L.va, c)
                if isinstance(c, int) and c == 1:
                    act.wait_ge(L.v_out, 16)
                act.activation(vt[:, :, :].rearrange("p j f -> p (j f)"), bank7[:, :], ACT.Copy).then_inc(L.v, 1)

        def act_square(act, L, c):
            if L.causal:
                act.wait_ge(L.turn, 14 * c + 3)
                act.activation(yb[:, :, :], ya[:, :, :], ACT.Square).then_inc(L.root, 1)

        def act_root(act, L, c):
            if L.causal:
                act.wait_ge(L.turn, 14 * c + 5)
                act.activation(root0[:, :], msq[:, :], ACT.Ln).then_inc(L.root, 1)
                act.wait_ge(L.root, 3 * c + 2)
                act.activation(root0[:, :], root0[:, :], ACT.Exp, scale=-0.5).then_inc(L.root, 1)

        def act_high(act, L, c, kq):
            if kq == 0:
                act.wait_ge(L.turn if L.causal else L.qk, 14 * c + 14 if L.causal else 2 * c + 2)
                after(act, L.kt_ps, 4 * c)
                after(act, L.qt_ps, 4 * c)
                if L.causal and isinstance(c, int) and c == 0:
                    act.wait_ge(x_loaded, 32)
            st = (KSt, QSt)[kq]
            act.activation(st[:, :, :, 0, :], heads_of(ya if L.causal else qk, kq), ACT.Copy).then_inc(L.parts, 1)

        def act_mid(act, L, c, kq):
            st = (KSt, QSt)[kq]
            act.wait_ge(L.rest, 8 * c + kq + 1)
            act.activation(st[:, :, :, 3 if kq == 0 else 1, :], heads_of(yb, kq), ACT.Copy).then_inc(L.parts, 1)

        def act_stacks(act, L, c, buf, steps=range(4)):
            for s in steps:
                j, h0 = s // 2, 8 * (s % 2)
                act.wait_ge(L.kt_ps, 4 * c + s + 1)
                if s == 0:
                    after(act, L.st_ps, HEADS * (c - 2))
                    if isinstance(c, int) and c == 2:
                        act.wait_ge(L.cls, 2)
                act.activation(KT[buf][:, h0:h0 + 8, 1 + j * P:1 + (j + 1) * P],
                               bank5[:, :].bitcast(BF16)[0:KS, :].rearrange("p (h q) -> p h q", q=P),
                               ACT.Copy).then_inc(L.kt, 1)

        def act_maxima(act, L, c, buf):
            act.wait_ge(L.m3_ps, c)
            after(act, L.st_ps, HEADS * (c - 2))
            act.activation(M3[buf][:, 1:T], bank6[:, :].bitcast(BF16)[0:KS, 0:SEQ], ACT.Copy).then_inc(L.m3, 1)

        def act_exp(act, L, c, h):
            n = HEADS * (c - 1) + h
            act.wait_ge(L.st_ps, n + 1)
            after(act, L.pv, GROUPS * (c - 1) + h // 4 - NPT // 4 + 1)
            if L.causal:
                n_t = SEQ + P
                e = act.activation(PT[h % NPT][:, :, :].rearrange("p i q -> p (i q)")[:, 0:n_t], psT[:, h % 4, 0:n_t], ACT.Exp)
            else:
                e = act.activation(PT[h % NPT][:, :, :], psT[:, 2 * (h % 2):2 * (h % 2) + 2, 0:T], ACT.Exp)
            e.then_inc(L.exp, 1)

        def act_out(act, L, c, g):
            act.wait_ge(L.pv, GROUPS * (c - 1) + g + 1)
            after(act, L.to_ps, 2 * (c - 1))
            after(act, L.otc, c - 1)
            act.activation(OT[:, g, :], bank4[:, 0:T], ACT.Copy).then_inc(L.ot_raw, 1)

        def act_onT(act, L, c):
            act.wait_ge(L.onT_ps, c)
            act.activation(ONT[:, :, :].rearrange("p k q -> p (k q)"), bank7[:, :], ACT.Copy).then_inc(L.onT, 1)

        def act_front(act, L, c):
            act_tokens(act, L, c)
            act_keys_queries(act, L, c, 0)
            act_keys_queries(act, L, c, 1)
            act_v(act, L, c)
            act_square(act, L, c)
            act_root(act, L, c)
            for kq in range(2):
                act_high(act, L, c, kq)
            for kq in range(2):
                act_mid(act, L, c, kq)
            if c == 0:
                act_stacks(act, L, c, 0)

        def act_round(act, L, k, buf, value=True, score=True, front=True, back=True):
            if value:
                act.wait_ge(L.sck_ps, k)
                after(act, L.pv, GROUPS * (k - 1))
                act.activation(EC[0:HEADS, :], bank7[0:HEADS, 0:T], ACT.Exp).then_inc(L.ec, 1)
            for h in range(HEADS):
                if value:
                    act_exp(act, L, k, h)
                    if h % 4 == 2 and h >= 6:
                        act_out(act, L, k, (h - 6) // 4)
                if score and h < 4:
                    act_stacks(act, L, k + 1, 1 - buf, [h])
                if front:
                    if h == L.s_front:
                        act_tokens(act, L, k + 2)
                    if h in (L.s_front + 1, L.s_front + 2):
                        act_keys_queries(act, L, k + 2, h - L.s_front - 1)
                    if h == L.s_front + 3:
                        act_v(act, L, k + 2)
                    if h == L.s_square:
                        act_square(act, L, k + 2)
                    if h == L.s_square + 2:
                        act_root(act, L, k + 2)
                if back and h == L.s_out + 3:
                    act_onT(act, L, k - 1)
                if front and h in (L.s_high, L.s_high + 1):
                    act_high(act, L, k + 2, h - L.s_high)
                if front and h in (L.s_high + 2, L.s_high + 3):
                    act_mid(act, L, k + 2, h - L.s_high - 2)
                if score and h == 15:
                    act_maxima(act, L, k + 1, 1 - buf)
            if value:
                act_out(act, L, k, 3)

        def act_attention(act, L):
            for c in range(2):
                act_front(act, L, c)
            rounds(act, L, act_round)
            act.wait_ge(L.onT_ps, B + 1)
            act.activation(ONT[:, 0:KC, 0:B], bank7[:, 0:KC * B].rearrange("p (k b) -> p k b", b=B), ACT.Copy).then_inc(L.onT, 1)

        def act_expert_tile(act, m, n):
            s = XB * m + n
            e = expert_of(act, s)
            after(act, m_midT_ps, 2 * (s - 1))
            for k, w in enumerate((w1a, w1b)):
                act.activation(w1s[n % 2][:, 2 * k:2 * k + 2, :],
                               w[:, bass.ds(e, 1), :].rearrange("p o (a f) -> p (o a) f", a=2), ACT.Copy).then_inc(m_w, 1)
            act.wait_ge(m_xT_ps, s + 1)
            act.activation(xT[n % 2][:, :, :].rearrange("p k q -> p (k q)"), bank(5 + n % 2)[:, 0:KC * P], ACT.Copy).then_inc(m_xT, 1)

        def tok_steps():
            yield "g0", 0, 0
            yield "g1", 0, 6
            yield "g2", 0, 7
            for k in range(6):
                yield "h", 1 << k, k

        def tok_operands(q, kind, width, k):
            def pick(ap):
                return ap.rearrange("p (j q g) -> p j q g", j=4, q=4)[:, :, q, :]
            G, H = (gre[q % 2], gim[q % 2]), (hre[q % 2], him[q % 2])
            if kind == "g0":
                x = tuple(cin[:, n, :, :].rearrange("p c (j q g) -> p q c j g", j=4, q=4)[:, q] for n in range(2))
                y = tuple(over(pick(zin[:, 3 + n, :]), 1, B) for n in range(2))
                o = tuple(g[:, :, 0, :].rearrange("p (j g) c -> p c j g", j=4) for g in G)
                return x, y, o, lambda t: t[:, 0:B * HC].rearrange("p (c j g) -> p c j g", c=B, j=4)
            zz = lambda n: pick(zn[:, k, :] if n == 2 else zp[:, n, k, :])
            if kind in ("g1", "g2"):
                w = B if kind == "g1" else 2 * B
                def rows_of(t, lo):
                    return t[:, :, :, :].rearrange("p (j g) a c -> p j g (a c)", j=4)[:, :, :, lo:lo + w]
                x = tuple(rows_of(g, 0) for g in G)
                y = tuple(over(zz(n), 3, w) for n in range(2))
                o = tuple(rows_of(g, w) for g in G)
            else:
                w = width
                def rows_of(t, lo):
                    return t[:, :, :].rearrange("p (j g) b -> p j g b", j=4)[:, :, :, lo:lo + w]
                x = tuple(rows_of(h, 0) for h in H)
                y = tuple(over(zz(n), 3, w) for n in (0, 2))
                o = tuple(rows_of(h, w) for h in H)
            return x, y, o, lambda t: t[:, 0:HC * w].rearrange("p (j g b) -> p j g b", j=4, g=8)

        def dve_norm_stats(dve, c, x, stat, mv, s_stat, s_mv):
            settle(dve)
            for j in range(2):
                dve.bn_stats(stat[:, j, :], x(j)).then_inc(s_stat, 1)
            dve.wait_ge(s_stat, 2 * c + 2)
            settle(dve)
            for j in range(2):
                dve.bn_aggr(mv[:, j, :], stat[:, j, :]).then_inc(s_mv, 1)

        def dve_norm_out(dve, c, x, o, mv, rstd, s_rstd, s_out):
            dve.wait_ge(s_rstd, 2 * c + 2)
            for j in range(2):
                dve.tensor_scalar(o(j), x(j), mv[:, j, 0:1], rstd[:, j, :], ALU.subtract, ALU.mult).then_inc(s_out, 1)

        def dve_stats(dve, L, c):
            if L.causal:
                dve_norm_stats(dve, c, lambda j: tile_x(c, j), stat, mv, L.stat, L.mv)
            else:
                dve_norm_stats(dve, c, lambda j: tile_x(c, j), stat2, mv2, L.stat_a, L.mv_a)

        def dve_norm_ahead(dve, L, c, step):
            if not L.causal and step == 0:
                dve_norm_out(dve, c, lambda j: tile_x(c, j), lambda j: tile_n(c, j), mv2, rstd2, L.rstd_a, L.x2)
            if not L.causal and step == 1:
                dve.wait_ge(L.x2, 2 * c + 2)
                dve_norm_stats(dve, c, lambda j: tile_n(c, j), stat, mv, L.stat, L.mv)

        def dve_norm(dve, L, c):
            after(dve, L.hnT_ps, c)
            x = tile_x if L.causal else tile_n
            dve_norm_out(dve, c, lambda j: x(c, j), lambda j: hn[:, j, :], mv, rstd, L.rstd, L.hn)

        def dve_keys_queries(dve, L, c, j):
            if not L.causal:
                dve.wait_ge(L.kq_ps, 2 * c + j + 1)
                if j == 0:
                    after(dve, L.parts, 4 * c)
                dve.tensor_tensor(qk[:, j, :], bank7[:, :], vecs[:, 0:2 * C], ALU.add).then_inc(L.qk, 1)

        def dve_v(dve, L, c):
            if not L.causal:
                dve.wait_ge(L.v_ps, c + 1)
                after(dve, L.va, c)
                if isinstance(c, int) and c == 1:
                    dve.wait_ge(L.v_out, 16)
                dve.tensor_tensor(vt[:, :, :], bank7[:, :].rearrange("p (j f) -> p j f", j=2),
                                  over(vecs[:, 2 * C:3 * C], 1, 2), ALU.add).then_inc(L.v, 1)

        def rope_table(name, c, d0, d1):
            first = 0 if isinstance(c, int) and c == 0 else 1
            t = tab(name).rearrange("p (k d) -> p k d", d=D)[:, first:first + 2, d0:d1]
            return over(t, 2, 2 * HEADS)

        def by_head(t):
            return t[:, :, :].rearrange("p j (h d) -> p j h d", d=D)

        def dve_turn(dve, L, c):
            if L.causal:
                dve.wait_ge(L.qk, 2 * c + 2)
                after(dve, L.rest, 8 * c)
                q, o, E2 = by_head(qk), by_head(yb), D // 2
                dve.tensor_tensor(o[:, :, :, 0:E2], q[:, :, :, E2:D], rope_table("sin", c, 0, E2), ALU.mult).then_inc(L.turn, 1)
                dve.tensor_tensor(o[:, :, :, E2:D], q[:, :, :, 0:E2], rope_table("sin", c, E2, D), ALU.mult).then_inc(L.turn, 1)

        def dve_squares(dve, L, c):
            if L.causal:
                dve.wait_ge(L.root, 3 * c + 1)
                dve.tensor_reduce(ss[:, :], yb[:, :, :].rearrange("p j (h d) -> p (j h) d", d=D), AX, ALU.add).then_inc(L.turn, 1)
                dve.wait_ge(L.turn, 14 * c + 4)
                dve.tensor_scalar(msq[:, :], ss[:, :], 1.0 / D, 1e-18, ALU.mult, ALU.max).then_inc(L.turn, 1)

        def dve_scale(dve, L, c):
            if L.causal:
                k = 14 * c
                dve.wait_ge(L.root, 3 * c + 3)
                dve.tensor_tensor(tmp[:, :], root0[:, :], root0[:, :], ALU.mult).then_inc(L.turn, 1)
                dve.wait_ge(L.turn, k + 6)
                dve.tensor_tensor(tmp[:, :], tmp[:, :], msq[:, :], ALU.mult).then_inc(L.turn, 1)
                dve.wait_ge(L.turn, k + 7)
                dve.tensor_scalar(tmp[:, :], tmp[:, :], -0.5, 1.5, ALU.mult, ALU.add).then_inc(L.turn, 1)
                dve.wait_ge(L.turn, k + 8)
                dve.tensor_tensor(tmp[:, :], tmp[:, :], root0[:, :], ALU.mult).then_inc(L.turn, 1)
                dve.wait_ge(L.turn, k + 9)
                dve.scalar_tensor_tensor(tmp[:, :], ss[:, :], 1.0 / D, tmp[:, :], ALU.mult, ALU.mult).then_inc(L.turn, 1)
                dve.wait_ge(L.turn, k + 10)
                dve.tensor_scalar(tmp[:, :], tmp[:, :], 1e-6, None, ALU.add).then_inc(L.turn, 1)
                dve.wait_ge(L.turn, k + 11)
                dve.reciprocal(ss[:, :], tmp[:, :]).then_inc(L.turn, 1)
                dve.wait_ge(L.turn, k + 12)
                dve.tensor_tensor(yb[:, :, :].rearrange("p j (h d) -> p (j h) d", d=D),
                                  ya[:, :, :].rearrange("p j (h d) -> p (j h) d", d=D),
                                  over(ss[:, :], 2, D), ALU.mult).then_inc(L.turn, 1)

        def dve_rest(dve, L, c, kq):
            y, st = ya if L.causal else qk, (KSt, QSt)[kq]
            dve.wait_ge(L.parts, 4 * c + kq + 1)
            if L.causal:
                dve.wait_ge(L.turn, 14 * c + 14)
            dve.tensor_tensor(heads_of(yb, kq), heads_of(y, kq), st[:, :, :, 0, :], ALU.subtract).then_inc(L.rest, 1)

        def dve_low(dve, L, c):
            k = 8 * c
            for kq, st in ((0, KSt), (1, QSt)):
                dve.wait_ge(L.parts, 4 * c + 2 + kq + 1)
                dve.wait_ge(L.rest, k + kq + 1)
                dve.tensor_tensor(st[:, :, :, 5 if kq == 0 else 2, :], heads_of(yb, kq),
                                  st[:, :, :, 3 if kq == 0 else 1, :], ALU.subtract).then_inc(L.rest, 1)
            dve.tensor_copy(KSt[:, :, :, 1:3, :].rearrange("p j h a d -> p (j h) a d"),
                            over(KSt[:, :, :, 0, :].rearrange("p j h d -> p (j h) d"), 2, 2)).then_inc(L.rest, 1)
            dve.tensor_copy(KSt[:, :, :, 4, :], KSt[:, :, :, 3, :]).then_inc(L.rest, 1)
            dve.tensor_copy(QSt[:, :, :, 3:5, :], QSt[:, :, :, 0:2, :]).then_inc(L.rest, 1)
            dve.tensor_copy(QSt[:, :, :, 5, :], QSt[:, :, :, 0, :]).then_inc(L.rest, 1)

        def dve_stacks(dve, L, c, buf, steps=range(4)):
            for s in steps:
                j, h0 = s // 2, 8 * (s % 2)
                dve.wait_ge(L.qt_ps, 4 * c + s + 1)
                if s == 0:
                    after(dve, L.st_ps, HEADS * (c - 2))
                    if isinstance(c, int) and c == 2:
                        dve.wait_ge(L.cls, 2)
                dve.tensor_copy(QT[buf][:, h0:h0 + 8, 1 + j * P:1 + (j + 1) * P],
                                bank6[:, :].bitcast(BF16)[0:KS, :].rearrange("p (h q) -> p h q", q=P)).then_inc(L.qt, 1)

        def dve_max(dve, L, c, h):
            dve.wait_ge(L.sq_ps, 32 * (c - 1) + 2 * h + 2)
            if L.causal:
                for j in range(2):
                    dve.tensor_reduce(NM[:, j, h:h + 1], score_ps(L, h, j), AX, ALU.max, negate=True).then_inc(L.mx, 1)
            else:
                dve.tensor_reduce(NM[:, :, h:h + 1], bank(5 + h % 2)[:, :].rearrange("p (j q) -> p j q", j=2),
                                  AX, ALU.max, negate=True).then_inc(L.mx, 2)

        def dve_maxima(dve, L, c):
            dve.wait_ge(L.mx, 32 * c)
            after(dve, L.m3_ps, c - 1)
            if not L.causal:
                dve.wait_ge(L.ck_ps, c)
                dve.scalar_tensor_tensor(NM[:, :, :], bank7[:, 0:2 * HEADS].rearrange("p (j h) -> p j h", j=2), -1.0,
                                         NM[:, :, :], ALU.mult, ALU.min).then_inc(L.ck, 1)
                dve.wait_ge(L.ck, c)
            ms = [MS[:, :, k, 0:HEADS] for k in range(3)]
            dve.tensor_copy(ms[0], NM[:, :, :]).then_inc(L.ms, 1)
            dve.wait_ge(L.ms, 4 * (c - 1) + 1)
            dve.tensor_tensor(NR[:, :, :], NM[:, :, :], ms[0], ALU.subtract).then_inc(L.ms, 1)
            dve.wait_ge(L.ms, 4 * (c - 1) + 2)
            dve.tensor_copy(ms[1], NR[:, :, :]).then_inc(L.ms, 1)
            dve.wait_ge(L.ms, 4 * (c - 1) + 3)
            dve.tensor_tensor(ms[2], NR[:, :, :], ms[1], ALU.subtract).then_inc(L.ms, 1)

        def dve_class_maxima(dve, L, c, buf):
            n = 1 if L.causal else T
            dve.wait_ge(L.scq_ps, c)
            after(dve, L.st_ps, HEADS * (c - 2))
            k = 6 * (c - 1)
            dve.tensor_reduce(NMC[:, :], bank5[0:HEADS, 0:n], AX, ALU.max, negate=True).then_inc(L.mc, 1)
            dve.wait_ge(L.mc, k + 1)
            dve.tensor_copy(M3[buf][0:HEADS, 0:1], NMC[:, :]).then_inc(L.mc, 1)
            dve.wait_ge(L.mc, k + 2)
            dve.tensor_tensor(NRC[:, :], NMC[:, :], M3[buf][0:HEADS, 0:1], ALU.subtract).then_inc(L.mc, 1)
            dve.wait_ge(L.mc, k + 3)
            dve.tensor_copy(MC[:, :], NRC[:, :]).then_inc(L.mc, 1)
            dve.wait_ge(L.mc, k + 4)
            dve.tensor_copy(M3[buf][32:32 + HEADS, 0:1], MC[:, :]).then_inc(L.mc, 1)
            dve.tensor_tensor(M3[buf][64:64 + HEADS, 0:1], NRC[:, :], MC[:, :], ALU.subtract).then_inc(L.mc, 1)

        def dve_out(dve, L, c, j, parts=P):
            n = 4 * (c - 1) + 2 * j
            dve.wait_ge(L.to_ps, 2 * (c - 1) + j + 1)
            after(dve, L.on, n)
            after(dve, L.onT_ps, c - 1)
            v = bank7[0:parts, :].rearrange("p (h d) -> p h d", d=32)
            dve.reciprocal(RZ[0:parts, :], v[:, :, D]).then_inc(L.on, 1)
            dve.wait_ge(L.on, n + 1)
            dve.tensor_tensor(ON[0:parts, j, :].rearrange("p (h d) -> p h d", d=D), v[:, :, 0:D],
                              over(RZ[0:parts, :], 2, D), ALU.mult).then_inc(L.on, 1)

        def dve_add(dve, L, c):
            o = C if L.causal else 0
            dve.wait_ge(L.pj_ps, c)
            t = rows[:, col(2 * c, 2), o:o + C]
            dve.tensor_tensor(t, t, bank7[:, :].rearrange("p (j f) -> p j f", j=2), ALU.add).then_inc(L.h, 1)

        def dve_second(dve, L, n):
            if not L.causal:
                c = 0 if isinstance(n, int) and n == B else n + 1
                dve.wait_ge(r_res, 2 * n + 1)
                dve_norm_stats(dve, n, lambda j: tile_n(c, j), stat3, mv3, r_stat, r_mv)

        def dve_second_out(dve, L, n):
            if not L.causal:
                c = 0 if isinstance(n, int) and n == B else n + 1
                dve.wait_ge(r_res, 2 * n + 2)
                dve_norm_out(dve, n, lambda j: tile_n(c, j), lambda j: tile_n(c, j), mv3, rstd3, r_rstd, r_hn)

        def dve_front(dve, L, c):
            dve_stats(dve, L, c)
            dve_norm_ahead(dve, L, c, 0)
            dve_norm_ahead(dve, L, c, 1)
            dve_norm(dve, L, c)
            dve_keys_queries(dve, L, c, 0)
            dve_keys_queries(dve, L, c, 1)
            dve_v(dve, L, c)
            dve_turn(dve, L, c)
            dve_squares(dve, L, c)
            dve_scale(dve, L, c)
            for kq in range(2):
                dve_rest(dve, L, c, kq)
            dve_low(dve, L, c)
            if c == 0:
                dve_stacks(dve, L, c, 0)

        def dve_round(dve, L, k, buf, value=True, score=True, front=True, back=True):
            if front:
                dve_stats(dve, L, k + 2)
            for h in range(HEADS):
                if front and h == L.s_norm:
                    dve_norm(dve, L, k + 2)
                if score and h < 4:
                    dve_stacks(dve, L, k + 1, 1 - buf, [h])
                if front and h in (1, 2):
                    dve_norm_ahead(dve, L, k + 2, h - 1)
                if score:
                    for hh in score_heads(h):
                        dve_max(dve, L, k + 1, hh)
                if front:
                    if h in (L.s_front + 1, L.s_front + 2):
                        dve_keys_queries(dve, L, k + 2, h - L.s_front - 1)
                    if h == L.s_front + 3:
                        dve_v(dve, L, k + 2)
                        dve_turn(dve, L, k + 2)
                if back and h in (L.s_out, L.s_out + 1):
                    dve_out(dve, L, k - 1, h - L.s_out)
                if front and h == L.s_square + 1:
                    dve_squares(dve, L, k + 2)
                if front and h == L.s_square + 3:
                    dve_scale(dve, L, k + 2)
                if back and h == L.s_out + 5:
                    dve_add(dve, L, k - 1)
                if back and h == 9:
                    dve_second(dve, L, k - 2)
                if back and h == 12:
                    dve_second_out(dve, L, k - 2)
                if score and h == 13:
                    dve_maxima(dve, L, k + 1)
                if score and h == 14:
                    dve_class_maxima(dve, L, k + 1, 1 - buf)
                if front and h in (L.s_high + 1, L.s_high + 2):
                    dve_rest(dve, L, k + 2, h - L.s_high - 1)
                if front and h == 15:
                    dve_low(dve, L, k + 2)

        def dve_attention(dve, L):
            dve.wait_ge(L.in_vec, 16)
            if not L.causal:
                dve.wait_ge(L.in_w, 32)
                dve.tensor_scalar(wqkv[:, :, C:2 * C], wqkv[:, :, C:2 * C], D ** -0.5, None, ALU.mult).then_inc(cleared, 1)
            dve.tensor_scalar(vecs[:, C:2 * C], vecs[:, C:2 * C], D ** -0.5, None, ALU.mult).then_inc(cleared, 1)
            dve.wait_ge(cleared, 13 if L.causal else 15)
            for c in range(2):
                if c == 1 and L.causal:
                    dve.wait_ge(x_loaded, 32)
                dve_front(dve, L, c)
            rounds(dve, L, dve_round)
            dve_out(dve, L, B + 1, 0, parts=B)
            dve.wait_ge(L.pj_ps, B + 1)
            o = C if L.causal else 0
            dve.tensor_tensor(rows[0:B, 0, o:o + C], rows[0:B, 0, o:o + C], bank7[0:B, 0:C], ALU.add).then_inc(L.h, 1)
            dve.wait_ge(L.h, B + 1)
            dve_second(dve, L, B)
            dve_second_out(dve, L, B)

        def dve_routing(dve):
            with dve.Fori(0, TILES // 2 // GP) as m:
                for n in range(GP):
                    dve.wait_ge(r_lg_ps, GP * m + n + 1)
                    dve.tensor_tensor(lg[:, bass.ds(2 * (GP * m + n), 2), :], psT[:, n, 0:2 * E].rearrange("p (j e) -> p j e", e=E),
                                      over(lnv[:, 3 * C:3 * C + E], 1, 2), ALU.add).then_inc(r_lg, 1)
            n_r = [0]

            def step(ins):
                ins.then_inc(r_step, 1)
                n_r[0] += 1
                dve.wait_ge(r_step, n_r[0])

            dve.wait_ge(r_lg, TILES // 2)
            step(dve.tensor_reduce(lmax[:, :], lg[:, :, :], AX, ALU.max))
            step(dve.tensor_tensor(lc[:, :, :], lg[:, :, :], over(lmax[:, :], 2, E), ALU.is_equal))
            step(dve.tensor_tensor(lc[:, :, :], lc[:, :, :], tab("prefer").rearrange("p (t e) -> p t e", e=E), ALU.mult))
            step(dve.tensor_reduce(lmax[:, :], lc[:, :, :], AX, ALU.max))
            step(dve.tensor_scalar(lmax[:, :], lmax[:, :], 1.0, None, ALU.max))
            step(dve.tensor_tensor(oh[:, :, :], lc[:, :, :], over(lmax[:, :], 2, E), ALU.is_equal))
            step(dve.tensor_tensor(oh[:, :, :], oh[:, :, :], over(tab("valid"), 2, E), ALU.mult))
            dve.wait_ge(r_cnt_ps, 1)
            step(dve.tensor_copy(tot[:, :, :], bank6[:, 0:TILES * E].rearrange("p (t e) -> p e t", e=E)))
            flat = lambda t: t[:, :, :].rearrange("p e t -> p (e t)")
            step(dve.tensor_tensor_scan(flat(cum), tab("restart"), flat(tot), 0.0, ALU.mult, ALU.add))
            bigv = big[:, :].rearrange("p (e k) -> p e k", e=E)
            step(dve.tensor_tensor(bigv, over(cum[:, :, TILES - 1], 2, TILES - 1),
                                   tab("full").rearrange("p (e k) -> p e k", e=E), ALU.is_gt))
            step(dve.tensor_reduce(nt[:, :], bigv, AX, ALU.add))
            step(dve.tensor_tensor_scan(ct[:, :], tab("ones")[:, 0:E], nt[:, :], 0.0, ALU.mult, ALU.add))
            step(dve.tensor_tensor(base[:, :], ct[:, :], nt[:, :], ALU.subtract))
            step(dve.tensor_scalar(base[:, :], base[:, :], float(P), None, ALU.mult))
            step(dve.tensor_tensor(tot[:, :, :], cum[:, :, :], tot[:, :, :], ALU.subtract))
            step(dve.tensor_tensor(tot[:, :, :], tot[:, :, :], over(base[:, :], 2, TILES), ALU.add))
            step(dve.tensor_tensor(lc[:, :, :], bank5[:, 0:TILES * E].rearrange("p (t e) -> p t e", e=E),
                                   tot[:, :, :].rearrange("p e t -> p t e"), ALU.add))
            step(dve.tensor_tensor(lc[:, :, :], lc[:, :, :], oh[:, :, :], ALU.mult))
            step(dve.tensor_reduce(slotf[:, :], lc[:, :, :], AX, ALU.add))
            dve.tensor_copy(slot[:, :], slotf[:, :]).then_inc(r_slot, 1)
            step(dve.tensor_tensor(exf[:, :, :], over(ct[:, :], 1, SLOT_TILES),
                                   tab("tile_no").rearrange("p (s e) -> p s e", e=E), ALU.is_le))
            step(dve.tensor_reduce(exr[:, :], exf[:, :, :], AX, ALU.add))
            dve.tensor_scalar(ex[:, :], exr[:, :], float(E - 1), None, ALU.min).then_inc(r_ex, 1)
            dve.wait_ge(r_ex, 1)

        def dve_result(dve, s, n):
            e = expert_of(dve, s)
            dve.wait_ge(m_y_ps, s + 1)
            dve.tensor_tensor(yo[n], bank(4 + 3 * (n % 2))[:, 0:C], b2r[:, bass.ds(e, 1), :].rearrange("p o f -> p (o f)"),
                              ALU.add).then_inc(m_yb, 1)
            dve.wait_ge(m_yb, s + 1)
            dve.tensor_tensor(yo[n], yo[n], xst[n][:, C:2 * C], ALU.add).then_inc(m_yo, 1)

        def dve_expert_tile(dve, m, n):
            s = XB * m + n
            e = expert_of(dve, s)
            after(dve, m_y_ps, s - 1)
            for k in range(FC):
                if k % 4 == 0:
                    dve.wait_ge(m_midT_ps, 2 * s + k // 4 + 1)
                dve.tensor_scalar(midT[n % 2][:, k // 4, k % 4, :], psT[:, 2 * (n % 2) + k // 4, (k % 4) * P:(k % 4 + 1) * P],
                                  b1t[:, bass.ds(e, 1), k], 0.0, ALU.add, ALU.max).then_inc(m_midT, 1)
            if not (isinstance(s, int) and s == 0):
                dve_result(dve, s - 1, (n - 1) % XB)

        def dve_experts(dve):
            dve.wait_ge(in_moe, 32)
            expert_tiles(dve, dve_expert_tile)
            dve_result(dve, SLOT_TILES - 1, XB - 1)

        def root(pool, c, ve, mv, half, rstd, s_mv, s_rstd, eps):
            pool.wait_ge(s_mv, 2 * c + 2)
            settle(pool)
            pool.tensor_scalar(ve[:, :, :], mv[:, :, 1:2], eps, None, ALU.add).then_inc(s_rstd, 1)
            pool.wait_ge(s_rstd, 2 * c + 1)
            pool.tensor_tensor(rstd[:, :, :], ve[:, :, :], half.unsqueeze(2), ALU.pow).then_inc(s_rstd, 1)

        def pool_norm(pool, L, c):
            if not L.causal:
                root(pool, c, ve2, mv2, half[:, :], rstd2, L.mv_a, L.rstd_a, 1e-5)
            root(pool, c, ve, mv, half[:, :], rstd, L.mv, L.rstd, 1e-5)
            if not L.causal:
                pool.wait_ge(L.hn, 2 * c + 2)
                settle(pool)
                pool.tensor_tensor(hn[:, :, :], hn[:, :, :], over(vecs[:, 3 * C:4 * C], 1, 2), ALU.mult).then_inc(L.hb, 1)
                pool.wait_ge(L.hb, 2 * c + 1)
                settle(pool)
                pool.tensor_tensor(hn[:, :, :], hn[:, :, :], over(vecs[:, 4 * C:5 * C], 1, 2), ALU.add).then_inc(L.hb, 1)

        def pool_turn(pool, L, c):
            if L.causal:
                pool.wait_ge(L.qk, 2 * c + 2)
                after(pool, L.rest, 8 * c)
                after(pool, L.parts, 4 * c)
                pool.tensor_tensor(by_head(ya), by_head(qk), rope_table("cos", c, 0, D), ALU.mult).then_inc(L.rc, 1)
                pool.wait_ge(L.turn, 14 * c + 2)
                pool.wait_ge(L.rc, c + 1)
                settle(pool)
                pool.tensor_tensor(ya[:, :, :], ya[:, :, :], yb[:, :, :], ALU.add).then_inc(L.turn, 1)
                pool.wait_ge(L.turn, 14 * c + 13)
                settle(pool)
                pool.tensor_tensor(ya[:, :, :], yb[:, :, :], over(vecs[:, 0:2 * C], 1, 2), ALU.mult).then_inc(L.turn, 1)

        def pool_values(pool, L, c, buf):
            pool.wait_ge(L.v, c + 1)
            after(pool, L.pv, GROUPS * (c - 2))
            settle(pool)
            pool.tensor_copy(VA[buf][:, :, :, 0:D], by_head(vt)).then_inc(L.va, 1)

        def pool_column(pool, L, c, buf):
            after(pool, L.st_ps, HEADS * (c - 2))
            after(pool, L.scq_ps, c - 1)
            settle(pool)
            pool.tensor_copy(KT[buf][:, :, 0:1], KTc[:, :, col(c - 1)]).then_inc(L.col0, 1)
            pool.tensor_copy(QT[buf][:, :, 0:1], QTc[:, :, col(c - 1)]).then_inc(L.col0, 1)
            pool.tensor_copy(QZ[:, :, HEADS - 1:HEADS], QTc[:, :, col(c - 1)]).then_inc(L.col0, 1)

        def pool_second(pool, L, n):
            if not L.causal:
                c = 0 if isinstance(n, int) and n == B else n + 1
                pool.wait_ge(L.h, n + 1)
                settle(pool)
                n2, x2 = rows[:, col(2 * c, 2), 0:C], rows[:, col(2 * c, 2), C:2 * C]
                pool.tensor_tensor(n2, n2, over(lnv[:, 2 * C:3 * C], 1, 2), ALU.add).then_inc(r_res, 1)
                pool.wait_ge(r_res, 2 * n + 1)
                settle(pool)
                pool.tensor_tensor(x2, x2, n2, ALU.add).then_inc(r_res, 1)
                root(pool, n, ve3, mv3, half[:, :], rstd3, r_mv, r_rstd, 1e-5)
                pool.wait_ge(r_hn, 2 * n + 2)
                settle(pool)
                pool.tensor_tensor(n2, n2, over(lnv[:, 0:C], 1, 2), ALU.mult).then_inc(r_hb, 1)
                pool.wait_ge(r_hb, 2 * n + 1)
                settle(pool)
                pool.tensor_tensor(n2, n2, over(lnv[:, C:2 * C], 1, 2), ALU.add).then_inc(r_hb, 1)

        def pool_class_key(pool, L, c):
            after(pool, L.sck_ps, c - 1)
            settle(pool)
            pool.tensor_copy(KZ[:, :, HEADS - 1:HEADS], KTc[:, :, col(c - 1)]).then_inc(L.vb, 1)

        def pool_class_value(pool, L, c):
            after(pool, L.pv, GROUPS * (c - 1))
            settle(pool)
            pool.tensor_tensor(VB[0:HEADS, :, 0:D], over(VC[:, col(c - 1), :].rearrange("p o d -> p (o d)"), 1, HEADS),
                               tab("own", HEADS).rearrange("p (h d) -> p h d", d=D), ALU.mult).then_inc(L.vb, 1)

        def pool_round(pool, L, k, buf, value=True, score=True, front=True, back=True):
            if value:
                pool_class_value(pool, L, k)
            if back:
                pool.wait_ge(L.ot_raw, GROUPS * (k - 1))
                settle(pool)
                pool.tensor_copy(OTc[:, :, col(k - 2)], OT[:, :, 0:1]).then_inc(L.otc, 1)
            if score:
                pool_column(pool, L, k + 1, 1 - buf)
                pool_class_key(pool, L, k + 1)
            if front:
                pool_norm(pool, L, k + 2)
                pool_turn(pool, L, k + 2)
            if back:
                pool_second(pool, L, k - 2)
            if front:
                pool_values(pool, L, k + 2, buf)

        def pool_attention(pool, L):
            pool.wait_ge(L.in_vec, 16)
            pool.wait_ge(cleared, 13 if L.causal else 15)
            pool.wait_ge(in_ln, 32)
            if L.causal:
                pool.memset(half[:, :], -0.5).then_inc(h_one, 1)
                pool.wait_ge(h_one, 5)
            for c in range(2):
                pool_norm(pool, L, c)
                pool_turn(pool, L, c)
                pool_values(pool, L, c, c)
                if c == 0:
                    pool.wait_ge(L.kt, 4)
                    pool.wait_ge(L.qt, 4)
                    pool.tensor_copy(KTc[:, :, :], KT[0][:, :, 1:1 + B]).then_inc(L.cls, 1)
                    pool.tensor_copy(QTc[:, :, :], QT[0][:, :, 1:1 + B]).then_inc(L.cls, 1)
                    pool.wait_ge(L.cls, 2)
            pool.wait_ge(L.vc, 16)
            rounds(pool, L, pool_round)
            pool_second(pool, L, B)

        def pool_scatter(pool):
            pool.wait_ge(r_slot, 1)
            pool.wait_ge(r_res, TILES)
            pool.wait_ge(in_cls, 32)
            pool.wait_ge(pad_stored, 16 * SLOT_TILES)
            for t in range(TILES):
                if t != 1:
                    n = B if t == 0 else P
                    pool.indirect_dma_start(out=x_sorted, out_offset=bass.IndirectOffsetOnAxis(ap=slot[0:n, t:t + 1], axis=0),
                                            in_=rows[0:n, t, :], in_offset=None).then_inc(sorted_out, 16)
            with pool.Fori(0, SLOT_TILES // XB) as m:
                for n in range(XB):
                    pool.wait_ge(m_yo, XB * m + n + 1)
                    settle(pool)
                    pool.indirect_dma_start(
                        out=out.rearrange("b t f -> (b t) f"),
                        out_offset=bass.IndirectOffsetOnAxis(ap=xst[n].bitcast(U32)[:, 2 * C:ROW], axis=0),
                        in_=yo[n], in_offset=None, bounds_check=B * T - 1, oob_is_err=False,
                    ).then_inc(m_out[n], 16)
            for n in range(XB):
                pool.wait_ge(m_out[n], 16 * (SLOT_TILES // XB))

        @block.tensor
        def _(pe):
            pe.wait_ge(in_tab, 16)
            for q in range(CH):
                pe.wait_ge(z_done, q + 1)
                pe.wait_ge(zi_done, q + 1)
                for n in range(2):
                    ps = bank5 if n == 0 else bank6
                    if q:
                        pe.wait_ge(x_sb, 2 * (q - 1) + n + 1)
                    v = ps[:, :].rearrange("p (g b) -> p g b", b=AB)
                    lo, hi = n * 64, n * 64 + 64
                    for g in range(8):
                        for part, (gg, hh) in enumerate(((gre, hre), (gim, him))):
                            for j in range(4):
                                r = 8 * j + g
                                mm = pe.matmul(v[32 * j:32 * j + 32, g, :],
                                               gg[q % 2][lo:hi, r, :, :].rearrange("p a c -> p (a c)"),
                                               hh[q % 2][lo:hi, r, :], start=(part == 0), stop=(part == 1),
                                               skip_group_check=True)
                    mm.then_inc(x_ps, 1)
            for L in layers:
                pe_attention(pe, L)
            pe_routing(pe)
            pe_experts(pe)

        @block.scalar
        def _(act):
            for q in range(CH):
                for n in range(2):
                    act.wait_ge(x_ps, 2 * q + n + 1)
                    act.activation(xs_sb[:, n, q, :, :].rearrange("p g b -> p (g b)"),
                                   (bank5 if n == 0 else bank6)[:, :], ACT.Copy).then_inc(x_sb, 1)
            store_rows(act, 1)
            load_rows(act, 1)
            for L in layers:
                act_attention(act, L)
            act.wait_ge(r_hb, TILES)
            with act.Fori(0, TILES // 2 // GP) as m:
                for n in range(GP):
                    act.activation(gn[n][:, :, :], rows[:, bass.ds(2 * (GP * m + n), 2), 0:C], ACT.Copy).then_inc(r_gn, 1)
                for n in range(GP):
                    act.wait_ge(r_gT_ps, GP * m + n + 1)
                    act.activation(gT[n][:, :, :].rearrange("p k q -> p (k q)"), bank(5 + n)[:, :], ACT.Copy).then_inc(r_gT, 1)
            act.wait_ge(r_ex, 1)
            act.wait_ge(in_w1, 32 * E)
            act.wait_ge(sorted_out, 16 * (TILES - 1))
            expert_tiles(act, act_expert_tile)

        @block.vector
        def _(dve):
            dve.memset(rows[:, 0:2, 0:2 * C], 0.0).then_inc(filled, 1)
            n_z = [0]

            def z(ins):
                ins.then_inc(z_step, 1)
                n_z[0] += 1
                dve.wait_ge(z_step, n_z[0])

            dve.wait_ge(in_z, 32)
            ex_r, ex_n, ex_p = zt[:, 0:2, :], zt[:, 2:4, :], zt[:, 4:6, :]
            ex_i = zt[:, 6:8, :].bitcast(I32)
            z(dve.tensor_scalar(ex_r, zin[:, 0:2, :], EXP_MIN, EXP_MAX, ALU.max, ALU.min))
            z(dve.tensor_scalar(ex_n, ex_r, 1 / float(np.log(2)), ROUND, ALU.mult, ALU.add))
            z(dve.tensor_scalar(ex_n, ex_n, ROUND, None, ALU.subtract))
            z(dve.scalar_tensor_tensor(ex_r, ex_n, -LN2_HIGH, ex_r, ALU.mult, ALU.add))
            dve.tensor_scalar(ex_i, ex_n, 127.0, None, ALU.add).then_inc(z_step, 1)
            n_z[0] += 1
            z(dve.scalar_tensor_tensor(ex_r, ex_n, -LN2_LOW, ex_r, ALU.mult, ALU.add))
            z(dve.tensor_scalar(ex_p, ex_r, 1 / 5040, None, ALU.mult))
            for n in (720, 120, 24, 6, 2, 1):
                z(dve.scalar_tensor_tensor(ex_p, ex_p, 1 / n, ex_r, ALU.add, ALU.mult))
            z(dve.tensor_scalar(ex_i, ex_i, 23, None, ALU.logical_shift_left))
            z(dve.scalar_tensor_tensor(ex_r, ex_p, 1.0, zt[:, 6:8, :], ALU.add, ALU.mult))
            dt, ea = zt[:, 0, :], zt[:, 1, :]
            ur, ui, den, num = (zt[:, k, :] for k in (2, 3, 4, 5))
            a, b = zt[:, 6, :], zt[:, 7, :]
            zr, zi = zp[:, 0, 0, :], zp[:, 1, 0, :]
            z(dve.scalar_tensor_tensor(ur, dt, -0.5, ea, ALU.mult, ALU.mult))
            z(dve.scalar_tensor_tensor(ui, dt, 0.5, zin[:, 2, :], ALU.mult, ALU.mult))
            z(dve.tensor_tensor(a, ur, ur, ALU.mult))
            z(dve.tensor_tensor(b, ui, ui, ALU.mult))
            z(dve.tensor_tensor(a, a, b, ALU.add))
            z(dve.tensor_scalar(num, a, -1.0, 1.0, ALU.mult, ALU.add))
            z(dve.tensor_scalar(den, ur, -1.0, 1.0, ALU.mult, ALU.add))
            z(dve.tensor_tensor(den, den, den, ALU.mult))
            z(dve.tensor_tensor(den, den, b, ALU.add))
            z(dve.reciprocal(den, den))
            z(dve.tensor_tensor(zr, num, den, ALU.mult))
            z(dve.scalar_tensor_tensor(zi, ui, 2.0, den, ALU.mult, ALU.mult))
            for k in range(8):
                zr, zi = zp[:, 0, k, :], zp[:, 1, k, :]
                if k:
                    pr, pi = zp[:, 0, k - 1, :], zp[:, 1, k - 1, :]
                    z(dve.tensor_tensor(a, pr, pr, ALU.mult))
                    z(dve.tensor_tensor(b, pi, pi, ALU.mult))
                    z(dve.tensor_tensor(zr, a, b, ALU.subtract))
                    z(dve.scalar_tensor_tensor(zi, pr, 2.0, pi, ALU.mult, ALU.mult))
                if k < 6:
                    z(dve.tensor_scalar(zn[:, k, :], zi, -1.0, None, ALU.mult))
            for n in range(2):
                dve.memset(hre[n][:, :, 0:1], 1.0).then_inc(h_one, 1)
            z(dve.tensor_scalar(zin[:, 3:5, :], zin[:, 3:5, :], 2.0, None, ALU.mult))
            n_d = 0
            for q in range(CH):
                for kind, width, k in tok_steps():
                    n = n_d + 1
                    if n > 2:
                        dve.wait_ge(pool_step, 2 * (n - 2))
                    if kind == "g0" and q >= 2:
                        dve.wait_ge(x_ps, 2 * (q - 1))
                    (xr, xi), (yr, yi), (o_r, o_i), shape = tok_operands(q, kind, width, k)
                    u1, u2, u3 = (shape(t) for t in (t1, t2, t3[n % 2]))
                    dve.tensor_tensor(u3, xr, yi, ALU.mult).then_inc(dve_step, 1)
                    dve.tensor_tensor(u1, xr, yr, ALU.mult).then_inc(z_step, 1)
                    if n > 1:
                        dve.wait_ge(pool_step, 2 * (n - 1))
                    dve.tensor_tensor(u2, xi, yi, ALU.mult).then_inc(z_step, 1)
                    n_z[0] += 2
                    dve.wait_ge(z_step, n_z[0])
                    if kind == "h" and width == 32:
                        dve.tensor_tensor(o_r, u1, u2, ALU.subtract).then_inc(z_done, 1)
                        dve.wait_ge(z_done, q + 1)
                    else:
                        z(dve.tensor_tensor(o_r, u1, u2, ALU.subtract))
                    n_d = n
            dve.wait_ge(x_ps, 2 * CH)
            dve.wait_ge(pad_stored, 16 * SLOT_TILES)
            dve.memset(MS[:, :, :, :], 0.0).then_inc(cleared, 1)
            dve.memset(EC[:, :], 0.0).then_inc(cleared, 1)
            for n in range(2):
                dve.memset(M3[n][:, :], 0.0).then_inc(cleared, 1)
                dve.memset(VA[n][:, :, :, :], 0.0).then_inc(cleared, 1)
            dve.memset(VB[:, :, :], 0.0).then_inc(cleared, 1)
            dve.memset(QZ[:, :, :], 0.0).then_inc(cleared, 1)
            dve.memset(KZ[:, :, :], 0.0).then_inc(cleared, 1)
            dve.wait_ge(cleared, 9)
            for n in range(2):
                dve.memset(VA[n][:, :, :, D:D + 1], 1.0).then_inc(cleared, 1)
            dve.tensor_copy(VB[0:HEADS, :, D:D + 1], tab("ident")[0:HEADS, 0:HEADS].unsqueeze(2)).then_inc(cleared, 1)
            dve.wait_ge(cleared, 12)
            dve.wait_ge(in_cls, 32)
            for L in layers:
                dve_attention(dve, L)
            dve_routing(dve)
            dve_experts(dve)

        @block.gpsimd
        def _(pool):
            pool.memset(pad[:, 0:2 * C], 0.0).then_inc(filled, 1)
            pool.memset(rows_i[:, 2, 2 * C:ROW], NO_ROW).then_inc(filled, 1)
            for n in range(2):
                pool.memset(him[n][:, :, 0:1], 0.0).then_inc(h_one, 1)
            pool.wait_ge(h_one, 4)
            n = 0
            for q in range(CH):
                for kind, width, k in tok_steps():
                    n += 1
                    (xr, xi), (yr, yi), (o_r, o_i), shape = tok_operands(q, kind, width, k)
                    u3, u4 = shape(t3[n % 2]), shape(t4)
                    if n > 1:
                        pool.wait_ge(pool_step, 2 * (n - 1))
                    else:
                        pool.wait_ge(dve_step, 1)
                    if kind == "g0" and q >= 2:
                        pool.wait_ge(x_ps, 2 * (q - 1))
                    pool.tensor_tensor(u4, xi, yr, ALU.mult).then_inc(pool_step, 1)
                    pool.wait_ge(pool_step, 2 * n - 1)
                    pool.wait_ge(dve_step, n)
                    pool.tensor_tensor(o_i, u3, u4, ALU.add).then_inc(pool_step, 1)
                pool.wait_ge(pool_step, 2 * n)
                pool.sem_inc(zi_done, 1)
            for L in layers:
                pool_attention(pool, L)
            pool_scatter(pool)



def kernel(**inputs):
    import concourse.bacc as _bacc
    import ml_dtypes
    from concourse.bass_utils import run_bass_kernel_spmd as _run

    a = {k: np.ascontiguousarray(v) for k, v in inputs.items()}

    def by_state(x):
        return x.reshape(2, P, NS).transpose(0, 2, 1).reshape(P, P)

    def rep(x):
        return np.broadcast_to(x.reshape(1, -1), (P, x.size))

    table, at, tableb, atb, out_row = constants()
    log_dt = np.broadcast_to(a["L0_tok_log_dt"][:, None], (2 * P, NS))
    b_ri, c_ri = a["L0_tok_B_ri"], a["x"]
    f = lambda k: a["L0_ffn_" + k]
    ker = dict(
        table=table, tableb=tableb.astype(ml_dtypes.bfloat16), out_row=out_row,
        z_in=np.stack([by_state(x) for x in (log_dt, a["L0_tok_inv_A_real"], a["L0_tok_A_imag"], b_ri[..., 0], b_ri[..., 1])], 1),
        c_in=np.stack([np.stack([by_state(c_ri[b, :, :, k]) for b in range(B)], 1) for k in range(2)], 1),
        cls=np.broadcast_to(a["cls_tok"].reshape(1, C), (B, C)),
        wqkv=np.stack([a["L0_attn_W_kqv"].T, np.concatenate([f("wk"), f("wq"), f("wv")], 1)]),
        wout=np.stack([a["L0_attn_W_proj"].T, f("wo")]),
        vecs=np.stack([
            np.concatenate([rep(np.tile(a["L0_attn_k_norm_w"], HEADS)), rep(np.tile(a["L0_attn_q_norm_w"], HEADS)),
                            np.zeros((P, 3 * C), np.float32)], 1),
            np.concatenate([rep(f(k)) for k in ("bk", "bq", "bv", "ln1_g", "ln1_b")], 1)]),
        lnv=np.concatenate([rep(f(k)) for k in ("ln2_g", "ln2_b", "bo", "gate_b")], 1),
        gate_w=f("gate_w"), w1=f("w1"), w2=f("w2"),
        b1t=f("b1").reshape(E, FC, P).transpose(2, 0, 1),
        b2r=np.broadcast_to(f("b2")[None], (P, E, C)),
    )
    nc = _bacc.Bacc("TRN2", target_bir_lowering=False, num_devices=1)
    arrays, args = {}, {}
    for k, v in ker.items():
        arrays["in_" + k] = np.ascontiguousarray(v)
        args[k] = nc.dram_tensor("in_" + k, v.shape, mybir.dt.from_np(v.dtype), kind="ExternalInput").ap()
    out = nc.dram_tensor("out", (B, T, C), F32, kind="ExternalOutput").ap()
    bass_vit_tower(nc, args, out, at, atb, table.shape[1], tableb.shape[1])
    r = _run(nc, [arrays], core_ids=[0])
    return r.results[0]["out"]
```

```python
from contextlib import ExitStack

import numpy as np

import concourse.bass as bass
from concourse import mybir

F32 = mybir.dt.float32
BF16 = mybir.dt.bfloat16
I32 = mybir.dt.int32
U32 = mybir.dt.uint32
ALU = mybir.AluOpType
ACT = mybir.ActivationFunctionType
AX = mybir.AxisListType.X

P = 128
B = 8
SEQ = 256
T = SEQ + 1
C = 256
HEADS = 16
D = C // HEADS
NS = 64
KC = C // P
TILES = 2 + B * SEQ // P
PARTS = 6
KS = PARTS * D
GROUPS = HEADS // 4
E = 8
F = 1024
FC = F // P
SLOT_TILES = 24
SLOTS = SLOT_TILES * P
ROW = 2 * C + 1
NEG = -1.0e30
NO_ROW = 1 << 20
AB, AA = 64, 4
CH = 4
EXP_MIN, EXP_MAX = -87.3, 88.7
ROUND = 1.5 * 2.0 ** 23
LN2_HIGH = 355.0 / 512
LN2_LOW = float(np.log(2)) - LN2_HIGH
HC = 32


def class_row(h):
    return 32 * (h // 4) + h % 4


def constants():
    p = np.arange(P)
    cols = {}
    cols["ident"] = np.eye(P)
    cols["before"] = (p[:, None] < p[None, :]) * 1.0
    cols["ones"] = np.ones((P, P))
    inv_freq = (1.0 / 10000.0 ** (np.arange(0, D, 2, dtype=np.float32) / np.float32(D))).astype(np.float32)
    pos = np.stack([np.zeros(P), 1 + p, 1 + P + p], 1).astype(np.float32)
    ang = (pos[:, :, None] * inv_freq).astype(np.float32)
    cos, sin = np.cos(ang), np.sin(ang)
    cols["cos"] = np.concatenate([cos, cos], -1).reshape(P, -1)
    cols["sin"] = np.concatenate([-sin, sin], -1).reshape(P, -1)
    h = np.arange(HEADS)
    own = np.zeros((P, HEADS, D))
    own[class_row(h), h] = 1
    cols["own"] = own.reshape(P, -1)
    valid = np.ones((P, TILES))
    valid[B:, 0] = 0
    valid[:, 1] = 0
    cols["valid"] = valid
    cols["prefer"] = np.tile(E - np.arange(E), (P, TILES))
    cols["full"] = np.tile(P * np.arange(TILES - 1), (P, E))
    cols["tile_no"] = np.tile(np.repeat(np.arange(SLOT_TILES), E), (P, 1))
    restart = np.ones((P, E, TILES))
    restart[:, :, 0] = 0
    cols["restart"] = restart.reshape(P, -1)
    at, off = {}, 0
    for k, v in cols.items():
        at[k] = (off, v.shape[1])
        off += v.shape[1]
    table = np.concatenate(list(cols.values()), 1).astype(np.float32)
    halfs = {}
    halfs["identb"] = np.eye(P)
    halfs["mask_q"] = np.where(p[None, :] > p[:, None], NEG, 0.0)
    halfs["mask_k"] = np.where(p[:, None] > p[None, :], NEG, 0.0)
    selc, sel = np.zeros((P, P)), np.zeros((P, HEADS, P))
    for part in range(3):
        selc[32 * part + h, class_row(h)] = 1
        sel[32 * part + h, h] = 1
    halfs["selc"] = selc
    halfs["sel"] = sel.reshape(P, -1)
    atb, off = {}, 0
    for k, v in halfs.items():
        atb[k] = (off, v.shape[1])
        off += v.shape[1]
    tableb = np.concatenate(list(halfs.values()), 1).astype(np.float32)
    out_row = np.full((P, TILES), NO_ROW)
    out_row[:B, 0] = np.arange(B) * T
    for b in range(B):
        for j in range(2):
            out_row[:, 2 + 2 * b + j] = b * T + 1 + j * P + p
    return table, at, tableb, atb, out_row.astype(np.int32)


def after(eng, semaphore, value):
    if not (isinstance(value, int) and value <= 0):
        eng.wait_ge(semaphore, value)


def col(x, n=1):
    return slice(x, x + n) if isinstance(x, int) else bass.ds(x, n)


def over(ap, axis, n):
    v = ap.unsqueeze(axis)
    shape = list(v.shape)
    shape[axis] = n
    return v.broadcast_to(shape)


class Layer:

    def __init__(self, name, causal):
        self.name, self.causal = name, causal
        self.s_norm = 1 if causal else 4
        self.s_front = 1 if causal else 7
        self.s_square = 6 if causal else None
        self.s_high, self.s_mid = 11, 15 if causal else 14
        self.s_out = 5 if causal else 1


def bass_vit_tower(nc, A, out, at, atb, n_table, n_tableb):
    ctx = ExitStack()
    with ctx:
        def sb(name, shape, dt=F32, where=None):
            return (where or ctx).enter_context(nc.sbuf_tensor(name, shape, dt))

        def sem(name):
            return ctx.enter_context(nc.semaphore(name))

        psT = ctx.enter_context(nc.psum_tensor("psT", [P, 4, 512], F32))
        bank4 = ctx.enter_context(nc.psum_tensor("bank4", [P, 512], F32))
        bank5 = ctx.enter_context(nc.psum_tensor("bank5", [P, 512], F32))
        bank6 = ctx.enter_context(nc.psum_tensor("bank6", [P, 512], F32))
        bank7 = ctx.enter_context(nc.psum_tensor("bank7", [P, 512], F32))

        x_seq = nc.dram_tensor("x_seq", [B, SEQ, C], F32, kind="Internal").ap()
        v_cls = [nc.dram_tensor(f"v_cls{n}", [B, C], F32, kind="Internal").ap() for n in range(2)]
        x_sorted = nc.dram_tensor("x_sorted", [SLOTS, ROW], F32, kind="Internal").ap()

        rows = sb("rows", [P, TILES, ROW])
        rows_i = rows[:, :, :].bitcast(I32)
        table = sb("table", [P, n_table])
        w1a = sb("w1a", [P, E, F])
        gate_in = sb("gate_in", [P, KC, E])
        lnv = sb("lnv", [P, 3 * C + E])
        stat3 = sb("stat3", [P, 2, 6])
        mv3 = sb("mv3", [P, 2, 2])
        ve3 = sb("ve3", [P, 2, 1])
        rstd3 = sb("rstd3", [P, 2, 1])
        half = sb("half", [P, 2])

        def tab(name, parts=P):
            o, n = at[name]
            return table[0:parts, o:o + n]

        ident = tab("ident")

        tok = ExitStack()
        zin = sb("zin", [P, 5, P], F32, tok)
        cin = sb("cin", [P, 2, B, P], F32, tok)
        zp = sb("zp", [P, 2, 8, P], F32, tok)
        zn = sb("zn", [P, 6, P], F32, tok)
        hre = [sb(f"hre{n}", [P, HC, AB], F32, tok) for n in range(2)]
        him = [sb(f"him{n}", [P, HC, AB], F32, tok) for n in range(2)]
        gre = [sb(f"gre{n}", [P, HC, AA, B], F32, tok) for n in range(2)]
        gim = [sb(f"gim{n}", [P, HC, AA, B], F32, tok) for n in range(2)]
        t1 = sb("t1", [P, HC * 32], F32, tok)
        t2 = sb("t2", [P, HC * 32], F32, tok)
        t3 = [sb(f"t3{n}", [P, HC * 32], F32, tok) for n in range(2)]
        t4 = sb("t4", [P, HC * 32], F32, tok)
        xs_sb = sb("xs_sb", [P, 2, CH, 8, AB], F32, tok)
        zt = t1[:, :].rearrange("p (k r) -> p k r", k=8)
        pad = rows[:, 2, :]
        tok.close()

        att = ExitStack()
        tableb = sb("tableb", [P, n_tableb], BF16, att)

        def tabb(name, parts=P):
            o, n = atb[name]
            return tableb[0:parts, o:o + n]

        identb = tabb("identb")
        wqkv = sb("wqkv", [P, KC, 3 * C], F32, att)
        wout = sb("wout", [P, KC, C], F32, att)
        vecs = sb("vecs", [P, 3 * C + 2 * C], F32, att)
        QT = [sb(f"QT{n}", [KS, HEADS, T], BF16, att) for n in range(2)]
        KT = [sb(f"KT{n}", [KS, HEADS, T], BF16, att) for n in range(2)]
        QTc = sb("QTc", [KS, HEADS, B], BF16, att)
        KTc = sb("KTc", [KS, HEADS, B], BF16, att)
        QZ = sb("QZ", [KS, HEADS, 31], BF16, att)
        KZ = sb("KZ", [KS, HEADS, 35], BF16, att)
        VA = [sb(f"VA{n}", [P, 2, HEADS, 32], F32, att) for n in range(2)]
        VC = sb("VC", [P, B, D], F32, att)
        VB = sb("VB", [P, HEADS, 32], F32, att)
        NM = sb("NM", [P, 2, HEADS], F32, att)
        NR = sb("NR", [P, 2, HEADS], F32, att)
        MS = sb("MS", [P, 2, 3, 32], BF16, att)
        NMC = sb("NMC", [HEADS, 1], F32, att)
        NRC = sb("NRC", [HEADS, 1], F32, att)
        MC = sb("MC", [HEADS, 1], BF16, att)
        M3 = [sb(f"M3{n}", [KS, T], BF16, att) for n in range(2)]
        EC = sb("EC", [P, T], F32, att)
        stat = sb("stat", [P, 2, 6], F32, att)
        mv = sb("mv", [P, 2, 2], F32, att)
        ve = sb("ve", [P, 2, 1], F32, att)
        rstd = sb("rstd", [P, 2, 1], F32, att)
        stat2 = sb("stat2", [P, 2, 6], F32, att)
        mv2 = sb("mv2", [P, 2, 2], F32, att)
        ve2 = sb("ve2", [P, 2, 1], F32, att)
        rstd2 = sb("rstd2", [P, 2, 1], F32, att)
        hn = sb("hn", [P, 2, C], F32, att)
        hnT = sb("hnT", [P, 4, P], F32, att)
        vt = sb("vt", [P, 2, C], F32, att)
        qk = sb("qk", [P, 2, 2 * C], F32, att)
        ya = sb("ya", [P, 2, 2 * C], F32, att)
        yb = sb("yb", [P, 2, 2 * C], F32, att)
        ss = sb("ss", [P, 64], F32, att)
        msq = sb("msq", [P, 64], F32, att)
        root0 = sb("root0", [P, 64], F32, att)
        tmp = sb("tmp", [P, 64], F32, att)
        KSt = sb("KSt", [P, 2, HEADS, PARTS, D], BF16, att)
        QSt = sb("QSt", [P, 2, HEADS, PARTS, D], BF16, att)
        NPT = 8
        PT = [sb(f"PT{n}", [P, 2, T], F32, att) for n in range(NPT)]
        OT = sb("OT", [P, GROUPS, T], F32, att)
        OTc = sb("OTc", [P, GROUPS, B], F32, att)
        RZ = sb("RZ", [P, HEADS], F32, att)
        ON = sb("ON", [P, 2, C], F32, att)
        ONT = sb("ONT", [P, 4, P], F32, att)
        att.close()

        moe = ctx
        w1b = sb("w1b", [P, E, F], F32, moe)
        w2 = sb("w2", [P, E, FC, C], F32, moe)
        b1t = sb("b1t", [P, E, FC], F32, moe)
        b2r = sb("b2r", [P, E, C], F32, moe)
        GP = 3
        gn = [sb(f"gn{n}", [P, 2, C], F32, moe) for n in range(GP)]
        gT = [sb(f"gT{n}", [P, 4, P], F32, moe) for n in range(GP)]
        lg = sb("lg", [P, TILES, E], F32, moe)
        lmax = sb("lmax", [P, TILES], F32, moe)
        lc = sb("lc", [P, TILES, E], F32, moe)
        oh = sb("oh", [P, TILES, E], F32, moe)
        tot = sb("tot", [P, E, TILES], F32, moe)
        cum = sb("cum", [P, E, TILES], F32, moe)
        nt = sb("nt", [P, E], F32, moe)
        big = sb("big", [P, E * (TILES - 1)], F32, moe)
        ct = sb("ct", [P, E], F32, moe)
        base = sb("base", [P, E], F32, moe)
        slotf = sb("slotf", [P, TILES], F32, moe)
        slot = sb("slot", [P, TILES], U32, moe)
        exf = sb("exf", [P, SLOT_TILES, E], F32, moe)
        exr = sb("exr", [P, SLOT_TILES], F32, moe)
        ex = sb("ex", [P, SLOT_TILES], I32, moe)
        XB = 4
        xst = [rows[:, n, :] for n in range(XB)]
        yo = [rows[:, 4 + n // 2, (n % 2) * C:(n % 2 + 1) * C] for n in range(XB)]
        midT = [rows[:, 6 + 2 * n:8 + 2 * n, 0:512].rearrange("p t (k q) -> p t k q", q=P) for n in range(2)]
        w1s = [rows[:, 10 + 4 * n:14 + 4 * n, 0:512] for n in range(2)]
        xT = [sb(f"xT{n}", [P, KC, P], F32, moe) for n in range(2)]

        in_tab = sem("in_tab"); in_z = sem("in_z"); in_cls = sem("in_cls")
        in_ln = sem("in_ln"); in_w1 = sem("in_w1"); in_w2 = sem("in_w2"); in_moe = sem("in_moe"); in_tabb = sem("in_tabb")
        filled = sem("filled"); pad_stored = sem("pad_stored")
        z_step = sem("z_step")
        h_one = sem("h_one")
        dve_step = sem("dve_step"); pool_step = sem("pool_step")
        x_ps = sem("x_ps"); x_sb = sem("x_sb"); x_stored = [sem(f"x_stored{n}") for n in range(2)]; x_loaded = sem("x_loaded")
        cleared = sem("cleared"); z_done = sem("z_done"); zi_done = sem("zi_done")

        layers = []
        for name, causal in (("a", True), ("b", False)):
            L = Layer(name, causal)
            L.in_w = sem(name + "_in_w"); L.in_wo = sem(name + "_in_wo"); L.in_vec = sem(name + "_in_vec")
            L.stat = sem(name + "_stat")
            L.mv = sem(name + "_mv"); L.rstd = sem(name + "_rstd"); L.hn = sem(name + "_hn")
            L.hnT_ps = sem(name + "_hnT_ps"); L.hnT = sem(name + "_hnT"); L.kq_ps = sem(name + "_kq_ps")
            L.qk = sem(name + "_qk"); L.v_ps = sem(name + "_v_ps"); L.v = sem(name + "_v"); L.va = sem(name + "_va")
            L.parts = sem(name + "_parts"); L.rest = sem(name + "_rest")
            L.kt_ps = sem(name + "_kt_ps"); L.qt_ps = sem(name + "_qt_ps"); L.kt = sem(name + "_kt")
            L.qt = sem(name + "_qt"); L.cls = sem(name + "_cls"); L.col0 = sem(name + "_col0")
            L.sq_ps = sem(name + "_sq_ps")
            L.mx = sem(name + "_mx"); L.ms = sem(name + "_ms"); L.scq_ps = sem(name + "_scq_ps")
            L.mc = sem(name + "_mc"); L.m3_ps = sem(name + "_m3_ps"); L.m3 = sem(name + "_m3")
            L.sck_ps = sem(name + "_sck_ps"); L.ec = sem(name + "_ec"); L.vb = sem(name + "_vb")
            L.st_ps = sem(name + "_st_ps"); L.exp = sem(name + "_exp"); L.pv = sem(name + "_pv")
            L.ot_raw = sem(name + "_ot_raw"); L.to_ps = sem(name + "_to_ps"); L.on = sem(name + "_on")
            L.onT_ps = sem(name + "_onT_ps"); L.onT = sem(name + "_onT"); L.otc = sem(name + "_otc")
            L.pj_ps = sem(name + "_pj_ps"); L.h = sem(name + "_h"); L.v_out = sem(name + "_v_out")
            L.vc = sem(name + "_vc")
            if causal:
                L.rc = sem(name + "_rc"); L.turn = sem(name + "_turn"); L.root = sem(name + "_root")
            else:
                L.ck_ps = sem(name + "_ck_ps"); L.ck = sem(name + "_ck")
                L.stat_a = sem(name + "_stat_a"); L.mv_a = sem(name + "_mv_a"); L.rstd_a = sem(name + "_rstd_a")
                L.x2 = sem(name + "_x2"); L.hb = sem(name + "_hb")
            layers.append(L)

        r_stat = sem("r_stat"); r_mv = sem("r_mv"); r_rstd = sem("r_rstd")
        r_res = sem("r_res"); r_hn = sem("r_hn"); r_hb = sem("r_hb"); r_gn = sem("r_gn")
        r_gT_ps = sem("r_gT_ps"); r_gT = sem("r_gT"); r_lg_ps = sem("r_lg_ps"); r_lg = sem("r_lg")
        r_step = sem("r_step"); r_cnt_ps = sem("r_cnt_ps"); r_slot = sem("r_slot")
        r_ex = sem("r_ex"); sorted_out = sem("sorted_out")
        m_x = [sem(f"m_x{n}") for n in range(XB)]
        m_xT_ps = sem("m_xT_ps"); m_xT = sem("m_xT"); m_w = sem("m_w")
        m_midT_ps = sem("m_midT_ps"); m_midT = sem("m_midT"); m_y_ps = sem("m_y_ps"); m_yb = sem("m_yb")
        m_yo = sem("m_yo")
        m_out = [sem(f"m_out{n}") for n in range(XB)]

        passed = sem("passed")

        def settle(eng):
            eng.sem_inc(passed, 1)

        def store_rows(eng, n):
            eng.wait_ge(x_sb, 2 * CH - 1 + n)
            for j in range(4):
                for a in range(AA):
                    lane = 32 * j + B * a
                    eng.dma_start(
                        x_seq[:, n * P + 32 * j:n * P + 32 * (j + 1), a * AB:(a + 1) * AB],
                        xs_sb[lane:lane + B, n, :, :, :].rearrange("c q g b -> c (q g) b"),
                    ).then_inc(x_stored[n], 16)

        def load_rows(eng, n):
            eng.wait_ge(x_stored[n], 16 * 4 * AA)
            eng.dma_start(rows[:, 2:TILES, C:2 * C].rearrange("p (c j) f -> p c j f", j=2)[:, :, n, :],
                          x_seq[:, n * P:(n + 1) * P, :].rearrange("c p f -> p c f")).then_inc(x_loaded, 16)

        block = ctx.enter_context(nc.Block())

        @block.sync
        def _(sp):
            sp.dma_start(zin[:, :, :], A["z_in"]).then_inc(in_z, 16)
            sp.dma_start(cin[:, :, :, :], A["c_in"]).then_inc(in_z, 16)
            sp.dma_start(table[:, :], A["table"]).then_inc(in_tab, 16)
            sp.wait_ge(filled, 3)
            for n in range(SLOT_TILES):
                sp.dma_start(x_sorted[n * P:(n + 1) * P, :], pad).then_inc(pad_stored, 16)
            sp.wait_ge(pad_stored, 16 * SLOT_TILES)
            sp.dma_start(rows_i[:, :, 2 * C:ROW], A["out_row"].unsqueeze(2), allow_slow_non_contiguous=True).then_inc(in_cls, 16)
            sp.dma_start(rows[0:B, 0, C:2 * C], A["cls"]).then_inc(in_cls, 16)
            sp.dma_start(lnv[:, :], A["lnv"]).then_inc(in_ln, 16)
            sp.dma_start(gate_in[:, :, :], A["gate_w"].rearrange("(k p) e -> p k e", p=P)).then_inc(in_ln, 16)
            for e in range(E):
                sp.dma_start(w1a[:, e, :], A["w1"][e, 0:P, :]).then_inc(in_w1, 16)
            sp.wait_ge(z_done, CH)
            sp.wait_ge(zi_done, CH)
            sp.dma_start(tableb[:, :], A["tableb"]).then_inc(in_tabb, 16)
            for n, L in enumerate(layers):
                if n:
                    sp.wait_ge(layers[0].v, B + 1)
                    sp.wait_ge(layers[0].turn, 12 * (B + 1))
                sp.dma_start(wqkv[:, :, :], A["wqkv"][n].rearrange("(k p) f -> p k f", p=P)).then_inc(L.in_w, 16)
                sp.dma_start(vecs[:, :], A["vecs"][n]).then_inc(L.in_vec, 16)
                if n:
                    sp.wait_ge(layers[0].h, B + 1)
                sp.dma_start(wout[:, :, :], A["wout"][n].rearrange("(k p) f -> p k f", p=P)).then_inc(L.in_wo, 16)
                if n == 0:
                    store_rows(sp, 0)
                    load_rows(sp, 0)
                sp.wait_ge(L.v, 1)
                sp.dma_start(v_cls[n].rearrange("b (h d) -> b h d", d=D),
                             vt[0:B, 0, :].rearrange("p (h d) -> p h d", d=D)).then_inc(L.v_out, 16)
                sp.wait_ge(L.v_out, 16)
                sp.wait_ge(cleared, 13)
                for k in range(4):
                    sp.dma_start(VC[32 * k:32 * k + 4, :, :],
                                 v_cls[n][:, 4 * k * D:4 * (k + 1) * D].rearrange("b (g d) -> g b d", d=D)).then_inc(L.vc, 16)
            L = layers[1]
            sp.wait_ge(L.h, B + 1)
            sp.wait_ge(L.otc, B)
            sp.dma_start(b1t[:, :, :], A["b1t"]).then_inc(in_moe, 16)
            sp.dma_start(b2r[:, :, :], A["b2r"]).then_inc(in_moe, 16)
            for e in range(E):
                sp.dma_start(w1b[:, e, :], A["w1"][e, P:C, :]).then_inc(in_w1, 16)
            for e in range(E):
                sp.dma_start(w2[:, e, :, :], A["w2"][e].rearrange("(k p) f -> p k f", p=P)).then_inc(in_w2, 16)
            sp.wait_ge(sorted_out, 16 * (TILES - 1))
            for n in range(XB):
                sp.dma_start(xst[n], x_sorted[n * P:(n + 1) * P, :]).then_inc(m_x[n], 16)
            with sp.Fori(1, SLOT_TILES // XB) as m:
                for n in range(XB):
                    sp.wait_ge(m_out[n], 16 * m)
                    sp.dma_start(xst[n], x_sorted[bass.ds((XB * m + n) * P, P), :]).then_inc(m_x[n], 16)

        def bank(n):
            return {4: bank4, 5: bank5, 6: bank6, 7: bank7}[n]

        def tile_x(c, j):
            return rows[:, col(2 * c + j), C:2 * C].rearrange("p o f -> p (o f)")

        def tile_n(c, j):
            return rows[:, col(2 * c + j), 0:C].rearrange("p o f -> p (o f)")

        def tiles_of(c):
            return 1 if isinstance(c, int) and c == 0 else 2

        def q_from(L, i):
            return 1 + i * P if L.causal else 0

        def score_ps(L, h, j):
            if L.causal:
                return bank(5 + h % 2)[:, j * (1 + P):j * (1 + P) + 1 + (j + 1) * P]
            return bank(5 + h % 2)[:, j * SEQ:(j + 1) * SEQ]

        def score_t_ps(L, h, i):
            if L.causal:
                return psT[:, h % 4, i * SEQ:i * SEQ + SEQ - i * P]
            return psT[:, 2 * (h % 2) + i, 0:T]

        def weights(L, h, i):
            if L.causal:
                return PT[h % NPT][:, :, :].rearrange("p i q -> p (i q)")[:, i * SEQ:i * SEQ + SEQ - i * P]
            return PT[h % NPT][:, i, 0:T]

        def expert_tiles(eng, one):
            for n in range(XB):
                one(eng, 0, n)
            with eng.Fori(1, SLOT_TILES // XB - 1) as m:
                for n in range(XB):
                    one(eng, m, n)
            for n in range(XB):
                one(eng, SLOT_TILES // XB - 1, n)

        def expert_of(eng, s):
            return eng.value_load(ex[0:1, col(s)], min_val=0, max_val=E - 1)

        def pe_turn_tokens(pe, L, c):
            pe.wait_ge(L.hn if L.causal else L.hb, 2 * c + 2)
            for j in range(tiles_of(c)):
                for k in range(KC):
                    mm = pe.transpose(bank7[:, (2 * j + k) * P:(2 * j + k + 1) * P], hn[:, j, k * P:(k + 1) * P], ident)
            mm.then_inc(L.hnT_ps, 1)

        def pe_keys_queries(pe, L, c, j):
            if j == 0:
                pe.wait_ge(L.hnT, c + 1)
            else:
                pe.wait_ge(L.qk, 2 * c + 1)
            for k in range(KC):
                mm = pe.matmul(bank7[:, :], hnT[:, 2 * j + k, :], wqkv[:, k, 0:2 * C], start=(k == 0), stop=(k == KC - 1))
            mm.then_inc(L.kq_ps, 3 - tiles_of(c))

        def pe_v(pe, L, c):
            for j in range(tiles_of(c)):
                for k in range(KC):
                    mm = pe.matmul(bank7[:, j * C:(j + 1) * C], hnT[:, 2 * j + k, :], wqkv[:, k, 2 * C:3 * C],
                                   start=(k == 0), stop=(k == KC - 1), skip_group_check=True)
            mm.then_inc(L.v_ps, 1)

        def stack_steps(c, s):
            return 3 if tiles_of(c) == 1 and s == 1 else 1

        def pe_stacks(pe, L, c, steps=range(4)):
            for s in steps:
                j, h0 = s // 2, 8 * (s % 2)
                for q, (st, ps, out_sem, used) in enumerate(((KSt, bank5, L.kt_ps, L.kt), (QSt, bank6, L.qt_ps, L.qt))):
                    if s == 0:
                        pe.wait_ge(L.rest, 8 * c + 6 + 2 * q)
                        after(pe, used, 4 * c)
                    else:
                        pe.wait_ge(used, 4 * c + s)
                    pv = ps[:, :].bitcast(BF16)
                    for n in range(8):
                        mm = pe.transpose(pv[0:KS, n * P:(n + 1) * P],
                                          st[:, j, h0 + n, :, :].rearrange("p a d -> p (a d)"), identb)
                    mm.then_inc(out_sem, stack_steps(c, s))

        def pe_scores(pe, L, c, buf, h):
            if h == 0:
                pe.wait_ge(L.kt, 4 * c + 4)
                pe.wait_ge(L.qt, 4 * c + 4)
                pe.wait_ge(L.col0, 3 * c)
            for j in range(2):
                if h >= 2 and j == 0:
                    pe.wait_ge(L.mx, 32 * (c - 1) + 2 * (h - 1))
                keys = slice(0, 1 + (j + 1) * P) if L.causal else slice(1, T)
                ps = score_ps(L, h, j)
                mm = pe.matmul(ps, QT[buf][:, h, 1 + j * P:1 + (j + 1) * P], KT[buf][:, h, keys],
                               start=True, stop=not L.causal, skip_group_check=True)
                if L.causal:
                    mm = pe.matmul(ps[:, 1 + j * P:1 + (j + 1) * P], identb, tabb("mask_q"),
                                   start=False, stop=True, skip_group_check=True)
                mm.then_inc(L.sq_ps, 1)

        def pe_class_scores(pe, L, c, buf):
            if not L.causal:
                for j in range(2):
                    for h in range(HEADS):
                        mm = pe.matmul(bank7[:, j * HEADS + h:j * HEADS + h + 1], QT[buf][:, h, 1 + j * P:1 + (j + 1) * P],
                                       KT[buf][:, h, 0:1], start=True, stop=True, skip_group_check=True)
                mm.then_inc(L.ck_ps, 1)

        def pe_class_queries(pe, L, c, buf):
            pe.wait_ge(L.mx, 32 * c)
            n = 1 if L.causal else T
            for h in range(HEADS):
                mm = pe.matmul(bank5[0:HEADS, 0:n], QZ[:, h, HEADS - 1 - h:2 * HEADS - 1 - h], KT[buf][:, h, 0:n],
                               start=(h == 0), stop=(h == HEADS - 1))
            mm.then_inc(L.scq_ps, 1)

        def pe_turn_maxima(pe, L, c):
            pe.wait_ge(L.ms, 4 * c)
            pv = bank6[:, :].bitcast(BF16)
            for j in range(2):
                mm = pe.transpose(pv[0:KS, j * P:(j + 1) * P], MS[:, j, :, :].rearrange("p a h -> p (a h)"), identb)
            mm.then_inc(L.m3_ps, 1)

        def pe_class_keys(pe, L, c, buf):
            pe.wait_ge(L.m3, c)
            pe.wait_ge(L.mc, 6 * c)
            pe.wait_ge(L.vb, 2 * c - 1)
            pe.matmul(bank7[:, 0:T], tabb("selc", KS), M3[buf][:, :], start=True, stop=False, skip_group_check=True)
            for g in range(4):
                for k in range(4):
                    mm = pe.matmul(bank7[32 * k:32 * k + 32, 0:T], KZ[:, 4 * k + g, 3 - g:35 - g], QT[buf][:, 4 * k + g, :],
                                   start=False, stop=(g == 3), skip_group_check=True)
            mm.then_inc(L.sck_ps, 1)

        def pe_scores_t(pe, L, c, buf, h):
            n = HEADS * (c - 1) + h
            after(pe, L.exp, n - 3 if L.causal else n - 1)
            for i in range(2):
                ps = score_t_ps(L, h, i)
                q0 = q_from(L, i)
                pe.matmul(ps, KT[buf][:, h, 1 + i * P:1 + (i + 1) * P], QT[buf][:, h, q0:T],
                          start=True, stop=False, skip_group_check=True)
                if L.causal:
                    pe.matmul(ps[:, 0:P], identb, tabb("mask_k"),
                              start=False, stop=False, skip_group_check=True)
                mm = pe.matmul(ps, tabb("sel", KS)[:, h * P:(h + 1) * P], M3[buf][:, q0:T],
                               start=False, stop=True, skip_group_check=True)
            mm.then_inc(L.st_ps, 1)

        def pe_values(pe, L, c, buf, g):
            if g == 0:
                pe.wait_ge(L.ec, c)
                pe.wait_ge(L.va, c + 1)
                pe.wait_ge(L.vb, 2 * c)
            after(pe, L.ot_raw, GROUPS * (c - 1) + g)
            pe.matmul(bank4[:, 0:T], VB[:, 4 * g:4 * g + 4, :].rearrange("p h d -> p (h d)"), EC[:, :],
                      start=True, stop=False, skip_group_check=True)
            pe.wait_ge(L.exp, HEADS * (c - 1) + 4 * g + 4)
            for i in range(2):
                q0 = q_from(L, i)
                for k in range(4):
                    h = 4 * g + k
                    mm = pe.matmul(bank4[32 * k:32 * k + 32, q0:T], VA[buf][:, i, h, :], weights(L, h, i),
                                   start=False, stop=(i == 1), skip_group_check=True)
            mm.then_inc(L.pv, 1)

        def pe_turn_out(pe, L, c, j):
            if j == 0:
                pe.wait_ge(L.ot_raw, GROUPS * c)
            else:
                pe.wait_ge(L.on, 4 * (c - 1) + 2)
            for g in range(GROUPS):
                mm = pe.transpose(bank7[:, g * P:(g + 1) * P], OT[:, g, 1 + j * P:1 + (j + 1) * P], ident)
            mm.then_inc(L.to_ps, 1)

        def pe_turn_on(pe, L, c):
            pe.wait_ge(L.on, 4 * c)
            for j in range(2):
                for k in range(KC):
                    mm = pe.transpose(bank7[:, (2 * j + k) * P:(2 * j + k + 1) * P], ON[:, j, k * P:(k + 1) * P], ident)
            mm.then_inc(L.onT_ps, 1)

        def pe_project(pe, L, c):
            pe.wait_ge(L.onT, c)
            for j in range(2):
                for k in range(KC):
                    mm = pe.matmul(bank7[:, j * C:(j + 1) * C], ONT[:, 2 * j + k, :], wout[:, k, :],
                                   start=(k == 0), stop=(k == KC - 1), skip_group_check=True)
            mm.then_inc(L.pj_ps, 1)

        def pe_fronts(pe, L):
            pe_turn_tokens(pe, L, 0)
            pe_keys_queries(pe, L, 0, 0)
            pe.wait_ge(L.qk, 2)
            pe_v(pe, L, 0)
            pe.wait_ge(L.v, 1)
            pe_turn_tokens(pe, L, 1)
            pe_keys_queries(pe, L, 1, 0)
            if not L.causal:
                pe_stacks(pe, L, 0, range(2))
            pe_keys_queries(pe, L, 1, 1)
            pe.wait_ge(L.qk, 4)
            pe_v(pe, L, 1)
            if L.causal:
                pe_stacks(pe, L, 0, range(2))

        def pe_round(pe, L, k, buf, value=True, score=True, front=True, back=True):
            if value:
                pe.wait_ge(L.v, min(k + 2, B + 1) if isinstance(k, int) else k + 2)
                if not L.causal:
                    pe.wait_ge(L.ck, k)
                if back:
                    after(pe, L.h, k - 2)
                pe_class_keys(pe, L, k, buf)
            for h in range(HEADS):
                if value:
                    pe_scores_t(pe, L, k, buf, h)
                if score and h < 4:
                    pe_stacks(pe, L, k + 1, [h])
                if score:
                    for hh in score_heads(h):
                        pe_scores(pe, L, k + 1, 1 - buf, hh)
                if value and h % 4 == 1 and h >= 5:
                    pe_values(pe, L, k, buf, (h - 5) // 4)
                if front and h == L.s_front:
                    if back and L.s_out < L.s_front:
                        pe.wait_ge(L.h, k - 1)
                    elif value:
                        pe.wait_ge(L.ec, k)
                    else:
                        pe.wait_ge(L.v, k + 2)
                    pe_turn_tokens(pe, L, k + 2)
                if front and h in (L.s_front + 1, L.s_front + 2):
                    pe_keys_queries(pe, L, k + 2, h - L.s_front - 1)
                if front and h == L.s_front + 3:
                    pe.wait_ge(L.qk, 2 * (k + 2) + 2)
                    pe_v(pe, L, k + 2)
                if back and h == L.s_out:
                    if front and L.s_front < L.s_out:
                        pe.wait_ge(L.v, k + 3)
                    elif value:
                        pe.wait_ge(L.ec, k)
                    else:
                        pe.wait_ge(L.h, k - 2)
                    pe_turn_out(pe, L, k - 1, 0)
                if back and h == L.s_out + 1:
                    pe_turn_out(pe, L, k - 1, 1)
                if back and h == L.s_out + 3:
                    pe_turn_on(pe, L, k - 1)
                if back and h == L.s_out + 5:
                    pe_project(pe, L, k - 1)
                if score and h == 12 and not L.causal:
                    if front:
                        pe.wait_ge(L.v, k + 3)
                    elif back:
                        pe.wait_ge(L.h, k - 1)
                    pe_class_scores(pe, L, k + 1, 1 - buf)
                if score and h == 14:
                    pe_class_queries(pe, L, k + 1, 1 - buf)
                if score and h == 15:
                    pe_turn_maxima(pe, L, k + 1)
            if value:
                pe_values(pe, L, k, buf, 3)

        def score_heads(h):
            return range(max(h - 4, 0) * 8 // 5 if h < 14 else HEADS, min(max(h - 3, 0) * 8 // 5, HEADS))

        def rounds(eng, L, one):
            one(eng, L, 0, 0, value=False, back=False)
            one(eng, L, 1, 1, back=False)
            with eng.Fori(0, 2) as m:
                one(eng, L, 2 * m + 2, 0)
                one(eng, L, 2 * m + 3, 1)
            one(eng, L, 6, 0)
            one(eng, L, 7, 1, front=False)
            one(eng, L, 8, 0, front=False, score=False)
            one(eng, L, 9, 1, front=False, score=False, value=False)

        def pe_attention(pe, L):
            pe.wait_ge(L.in_w, 16)
            pe.wait_ge(in_tabb, 16)
            pe_fronts(pe, L)
            pe.wait_ge(cleared, 13)
            pe.wait_ge(L.in_wo, 16)
            rounds(pe, L, pe_round)
            pe.wait_ge(L.otc, B)
            pe.wait_ge(L.h, B)
            for g in range(GROUPS):
                mm = pe.transpose(bank7[0:B, g * P:(g + 1) * P], OTc[:, g, :], ident)
            mm.then_inc(L.to_ps, 1)
            pe.wait_ge(L.on, 4 * B + 2)
            for k in range(KC):
                mm = pe.transpose(bank7[:, k * B:(k + 1) * B], ON[0:B, 0, k * P:(k + 1) * P], ident[0:B, 0:B])
            mm.then_inc(L.onT_ps, 1)
            pe.wait_ge(L.onT, B + 1)
            for k in range(KC):
                mm = pe.matmul(bank7[0:B, 0:C], ONT[:, k, 0:B], wout[:, k, :], start=(k == 0), stop=(k == KC - 1))
            mm.then_inc(L.pj_ps, 1)

        def pe_routing(pe):
            pe.wait_ge(in_ln, 32)
            with pe.Fori(0, TILES // 2 // GP) as m:
                for n in range(GP):
                    pe.wait_ge(r_gn, GP * m + n + 1)
                    for j in range(2):
                        for k in range(KC):
                            mm = pe.transpose(bank(5 + n)[:, (2 * j + k) * P:(2 * j + k + 1) * P],
                                              gn[n][:, j, k * P:(k + 1) * P], ident)
                    mm.then_inc(r_gT_ps, 1)
                for n in range(GP):
                    pe.wait_ge(r_gT, GP * m + n + 1)
                    for j in range(2):
                        for k in range(KC):
                            mm = pe.matmul(psT[:, n, j * E:(j + 1) * E], gT[n][:, 2 * j + k, :], gate_in[:, k, :],
                                           start=(k == 0), stop=(k == KC - 1), skip_group_check=True)
                    mm.then_inc(r_lg_ps, 1)
                pe.wait_ge(r_lg, GP * m + GP)
            pe.wait_ge(r_step, 7)
            flat = oh[:, :, :].rearrange("p t e -> p (t e)")
            pe.matmul(bank5[:, 0:TILES * E], tab("before"), flat, start=True, stop=True)
            pe.matmul(bank6[:, 0:TILES * E], tab("ones"), flat, start=True, stop=True).then_inc(r_cnt_ps, 1)

        def pe_sorted_turn(pe, m, n):
            pe.wait_ge(m_x[n], 16 * m + 16)
            for k in range(KC):
                mm = pe.transpose(bank(5 + n % 2)[:, k * P:(k + 1) * P], xst[n][:, k * P:(k + 1) * P], ident)
            mm.then_inc(m_xT_ps, 1)

        def pe_hidden(pe, s, n):
            pe.wait_ge(m_w, 2 * s + 2)
            pe.wait_ge(m_xT, s + 1)
            after(pe, m_midT, FC * (s - 1))
            for f in range(FC):
                for k in range(KC):
                    mm = pe.matmul(psT[:, 2 * (n % 2) + f // 4, (f % 4) * P:(f % 4 + 1) * P],
                                   w1s[n % 2][:, 2 * k + f // 4, (f % 4) * P:(f % 4 + 1) * P],
                                   xT[n % 2][:, k, :], start=(k == 0), stop=(k == KC - 1), skip_group_check=True)
                if f % 4 == 3:
                    mm.then_inc(m_midT_ps, 1)

        def pe_result(pe, s, n):
            e = expert_of(pe, s)
            after(pe, m_yb, s - 1)
            for k in range(FC):
                pe.wait_ge(m_midT, FC * s + k + 1)
                mm = pe.matmul(bank(4 + 3 * (n % 2))[:, 0:C], midT[n % 2][:, k // 4, k % 4, :],
                               w2[:, bass.ds(e, 1), k, :].rearrange("p o f -> p (o f)"),
                               start=(k == 0), stop=(k == FC - 1))
            mm.then_inc(m_y_ps, 1)

        def pe_expert_tile(pe, m, n):
            s = XB * m + n
            if not (isinstance(s, int) and s == SLOT_TILES - 1):
                pe_sorted_turn(pe, m + (n + 1) // XB, (n + 1) % XB)
            pe_hidden(pe, s, n)
            if not (isinstance(s, int) and s == 0):
                pe_result(pe, s - 1, (n - 1) % XB)

        def pe_experts(pe):
            pe.wait_ge(r_ex, 1)
            pe.wait_ge(r_slot, 1)
            pe.wait_ge(in_w1, 32 * E)
            pe.wait_ge(in_w2, 16 * E)
            pe_sorted_turn(pe, 0, 0)
            expert_tiles(pe, pe_expert_tile)
            pe_result(pe, SLOT_TILES - 1, XB - 1)

        def heads_of(y, kq):
            return y[:, :, kq * C:(kq + 1) * C].rearrange("p j (h d) -> p j h d", d=D)

        def act_tokens(act, L, c):
            act.wait_ge(L.hnT_ps, c + 1)
            n = tiles_of(c)
            act.activation(hnT[:, 0:2 * n, :].rearrange("p k q -> p (k q)"), bank7[:, 0:2 * n * P],
                           ACT.Copy).then_inc(L.hnT, 1)

        def act_keys_queries(act, L, c, j):
            if L.causal:
                act.wait_ge(L.kq_ps, 2 * c + j + 1)
                if j == 0:
                    after(act, L.turn, 12 * c - 10)
                    after(act, L.rc, c)
                act.activation(qk[:, j, :], bank7[:, :], ACT.Copy).then_inc(L.qk, 3 - tiles_of(c))

        def act_v(act, L, c):
            if L.causal:
                act.wait_ge(L.v_ps, c + 1)
                after(act, L.va, c)
                if isinstance(c, int) and c == 1:
                    act.wait_ge(L.v_out, 16)
                n = tiles_of(c)
                act.activation(vt[:, 0:n, :].rearrange("p j f -> p (j f)"), bank7[:, 0:n * C],
                               ACT.Copy).then_inc(L.v, 1)

        def act_square(act, L, c):
            if L.causal:
                act.wait_ge(L.turn, 12 * c + 3)
                act.activation(yb[:, 0:tiles_of(c), :], ya[:, 0:tiles_of(c), :], ACT.Square).then_inc(L.root, 1)

        def act_root(act, L, c):
            if L.causal:
                act.wait_ge(L.turn, 12 * c + 5)
                act.activation(root0[:, 0:32 * tiles_of(c)], msq[:, 0:32 * tiles_of(c)], ACT.Sqrt).then_inc(L.root, 1)

        def act_high(act, L, c, kq):
            if kq == 0:
                act.wait_ge(L.turn if L.causal else L.qk, 12 * c + 12 if L.causal else 2 * c + 2)
                after(act, L.kt_ps, 4 * c)
                after(act, L.qt_ps, 4 * c)
                if L.causal and isinstance(c, int) and c == 0:
                    act.wait_ge(x_loaded, 32)
            st = (KSt, QSt)[kq]
            n = tiles_of(c)
            act.activation(st[:, 0:n, :, 0, :], heads_of(ya if L.causal else qk, kq)[:, 0:n],
                           ACT.Copy).then_inc(L.parts, 1)

        def act_mid(act, L, c, kq):
            st = (KSt, QSt)[kq]
            act.wait_ge(L.rest, 8 * c + kq + 1)
            n = tiles_of(c)
            act.activation(st[:, 0:n, :, 3 if kq == 0 else 1, :], heads_of(yb, kq)[:, 0:n],
                           ACT.Copy).then_inc(L.parts, 1)

        def act_stacks(act, L, c, buf, steps=range(4)):
            for s in steps:
                j, h0 = s // 2, 8 * (s % 2)
                act.wait_ge(L.kt_ps, 4 * c + s + 1)
                if s == 0:
                    after(act, L.st_ps, HEADS * (c - 2))
                    if isinstance(c, int) and c == 2:
                        act.wait_ge(L.cls, 2)
                act.activation(KT[buf][:, h0:h0 + 8, 1 + j * P:1 + (j + 1) * P],
                               bank5[:, :].bitcast(BF16)[0:KS, :].rearrange("p (h q) -> p h q", q=P),
                               ACT.Copy).then_inc(L.kt, stack_steps(c, s))

        def act_maxima(act, L, c, buf):
            act.wait_ge(L.m3_ps, c)
            after(act, L.st_ps, HEADS * (c - 2))
            act.activation(M3[buf][:, 1:T], bank6[:, :].bitcast(BF16)[0:KS, 0:SEQ], ACT.Copy).then_inc(L.m3, 1)

        def act_exp(act, L, c, h):
            n = HEADS * (c - 1) + h
            act.wait_ge(L.st_ps, n + 1)
            after(act, L.pv, GROUPS * (c - 1) + h // 4 - NPT // 4 + 1)
            if L.causal:
                n_t = SEQ + P
                e = act.activation(PT[h % NPT][:, :, :].rearrange("p i q -> p (i q)")[:, 0:n_t], psT[:, h % 4, 0:n_t], ACT.Exp)
            else:
                e = act.activation(PT[h % NPT][:, :, :], psT[:, 2 * (h % 2):2 * (h % 2) + 2, 0:T], ACT.Exp)
            e.then_inc(L.exp, 1)

        def act_out(act, L, c, g):
            act.wait_ge(L.pv, GROUPS * (c - 1) + g + 1)
            after(act, L.to_ps, 2 * (c - 1))
            after(act, L.otc, c - 1)
            act.activation(OT[:, g, :], bank4[:, 0:T], ACT.Copy).then_inc(L.ot_raw, 1)

        def act_onT(act, L, c):
            act.wait_ge(L.onT_ps, c)
            act.activation(ONT[:, :, :].rearrange("p k q -> p (k q)"), bank7[:, :], ACT.Copy).then_inc(L.onT, 1)

        def act_fronts(act, L):
            act_tokens(act, L, 0)
            act_keys_queries(act, L, 0, 0)
            act_v(act, L, 0)
            act_square(act, L, 0)
            act_tokens(act, L, 1)
            act_root(act, L, 0)
            act_keys_queries(act, L, 1, 0)
            for kq in range(2):
                act_high(act, L, 0, kq)
            act_keys_queries(act, L, 1, 1)
            for kq in range(2):
                act_mid(act, L, 0, kq)
            act_v(act, L, 1)
            act_stacks(act, L, 0, 0, range(2))
            act_square(act, L, 1)
            act_root(act, L, 1)
            for kq in range(2):
                act_high(act, L, 1, kq)
            for kq in range(2):
                act_mid(act, L, 1, kq)

        def act_round(act, L, k, buf, value=True, score=True, front=True, back=True):
            if value:
                act.wait_ge(L.sck_ps, k)
                after(act, L.pv, GROUPS * (k - 1))
                act.activation(EC[:, :], bank7[:, 0:T], ACT.Exp).then_inc(L.ec, 1)
            for h in range(HEADS):
                if value:
                    act_exp(act, L, k, h)
                    if h % 4 == 2 and h >= 6:
                        act_out(act, L, k, (h - 6) // 4)
                if score and h < 4:
                    act_stacks(act, L, k + 1, 1 - buf, [h])
                if front:
                    if h == L.s_front:
                        act_tokens(act, L, k + 2)
                    if h in (L.s_front + 1, L.s_front + 2):
                        act_keys_queries(act, L, k + 2, h - L.s_front - 1)
                    if h == L.s_front + 3:
                        act_v(act, L, k + 2)
                    if L.causal and h == L.s_square:
                        act_square(act, L, k + 2)
                    if L.causal and h == L.s_square + 2:
                        act_root(act, L, k + 2)
                if back and h == L.s_out + 3:
                    act_onT(act, L, k - 1)
                if front and h in (L.s_high, L.s_high + 1):
                    act_high(act, L, k + 2, h - L.s_high)
                if front and h == L.s_mid:
                    for kq in range(2):
                        act_mid(act, L, k + 2, kq)
                if score and h == 15:
                    act_maxima(act, L, k + 1, 1 - buf)
            if value:
                act_out(act, L, k, 3)

        def act_attention(act, L):
            act_fronts(act, L)
            rounds(act, L, act_round)
            act.wait_ge(L.onT_ps, B + 1)
            act.activation(ONT[:, 0:KC, 0:B], bank7[:, 0:KC * B].rearrange("p (k b) -> p k b", b=B), ACT.Copy).then_inc(L.onT, 1)

        def act_expert_tile(act, m, n):
            s = XB * m + n
            e = expert_of(act, s)
            after(act, m_midT_ps, 2 * (s - 1))
            for k, w in enumerate((w1a, w1b)):
                act.activation(w1s[n % 2][:, 2 * k:2 * k + 2, :],
                               w[:, bass.ds(e, 1), :].rearrange("p o (a f) -> p (o a) f", a=2), ACT.Copy).then_inc(m_w, 1)
            act.wait_ge(m_xT_ps, s + 1)
            act.activation(xT[n % 2][:, :, :].rearrange("p k q -> p (k q)"), bank(5 + n % 2)[:, 0:KC * P],
                           ACT.Copy).then_inc(m_xT, 1)

        def tok_steps():
            yield "g0", 0, 0
            yield "g1", 0, 6
            yield "g2", 0, 7
            for k in range(6):
                yield "h", 1 << k, k

        def tok_operands(q, kind, width, k):
            def pick(ap):
                return ap.rearrange("p (j q g) -> p j q g", j=4, q=4)[:, :, q, :]
            G, H = (gre[q % 2], gim[q % 2]), (hre[q % 2], him[q % 2])
            if kind == "g0":
                x = tuple(cin[:, n, :, :].rearrange("p c (j q g) -> p q c j g", j=4, q=4)[:, q] for n in range(2))
                y = tuple(over(pick(zin[:, 3 + n, :]), 1, B) for n in range(2))
                o = tuple(g[:, :, 0, :].rearrange("p (j g) c -> p c j g", j=4) for g in G)
                return x, y, o, lambda t: t[:, 0:B * HC].rearrange("p (c j g) -> p c j g", c=B, j=4)
            zz = lambda n: pick(zn[:, k, :] if n == 2 else zp[:, n, k, :])
            if kind in ("g1", "g2"):
                w = B if kind == "g1" else 2 * B
                def rows_of(t, lo):
                    return t[:, :, :, :].rearrange("p (j g) a c -> p j g (a c)", j=4)[:, :, :, lo:lo + w]
                x = tuple(rows_of(g, 0) for g in G)
                y = tuple(over(zz(n), 3, w) for n in range(2))
                o = tuple(rows_of(g, w) for g in G)
            else:
                w = width
                def rows_of(t, lo):
                    return t[:, :, :].rearrange("p (j g) b -> p j g b", j=4)[:, :, :, lo:lo + w]
                x = tuple(rows_of(h, 0) for h in H)
                y = tuple(over(zz(n), 3, w) for n in (0, 2))
                o = tuple(rows_of(h, w) for h in H)
            return x, y, o, lambda t: t[:, 0:HC * w].rearrange("p (j g b) -> p j g b", j=4, g=8)

        def dve_norm_stats(dve, c, x, stat, mv, s_stat, s_mv):
            settle(dve)
            for j in range(2):
                dve.bn_stats(stat[:, j, :], x(j)).then_inc(s_stat, 1)
            dve.wait_ge(s_stat, 2 * c + 2)
            settle(dve)
            for j in range(2):
                dve.bn_aggr(mv[:, j, :], stat[:, j, :]).then_inc(s_mv, 1)

        def dve_norm_out(dve, c, x, o, mv, rstd, s_rstd, s_out):
            dve.wait_ge(s_rstd, 2 * c + 2)
            for j in range(2):
                dve.tensor_scalar(o(j), x(j), mv[:, j, 0:1], rstd[:, j, :], ALU.subtract, ALU.mult).then_inc(s_out, 1)

        def dve_stats(dve, L, c):
            if L.causal:
                dve_norm_stats(dve, c, lambda j: tile_x(c, j), stat, mv, L.stat, L.mv)
            else:
                dve_norm_stats(dve, c, lambda j: tile_x(c, j), stat2, mv2, L.stat_a, L.mv_a)

        def dve_norm_ahead(dve, L, c, step):
            if not L.causal and step == 0:
                dve_norm_out(dve, c, lambda j: tile_x(c, j), lambda j: tile_n(c, j), mv2, rstd2, L.rstd_a, L.x2)
            if not L.causal and step == 1:
                dve.wait_ge(L.x2, 2 * c + 2)
                dve_norm_stats(dve, c, lambda j: tile_n(c, j), stat, mv, L.stat, L.mv)

        def dve_norm(dve, L, c):
            after(dve, L.hnT_ps, c)
            x = tile_x if L.causal else tile_n
            dve_norm_out(dve, c, lambda j: x(c, j), lambda j: hn[:, j, :], mv, rstd, L.rstd, L.hn)

        def dve_keys_queries(dve, L, c, j):
            if not L.causal:
                dve.wait_ge(L.kq_ps, 2 * c + j + 1)
                if j == 0:
                    after(dve, L.parts, 4 * c)
                    after(dve, L.rest, 8 * c)
                dve.tensor_tensor(qk[:, j, :], bank7[:, :], vecs[:, 0:2 * C], ALU.add).then_inc(L.qk, 3 - tiles_of(c))

        def dve_v(dve, L, c):
            if not L.causal:
                dve.wait_ge(L.v_ps, c + 1)
                after(dve, L.va, c)
                if isinstance(c, int) and c == 1:
                    dve.wait_ge(L.v_out, 16)
                n = tiles_of(c)
                dve.tensor_tensor(vt[:, 0:n, :], bank7[:, 0:n * C].rearrange("p (j f) -> p j f", j=n),
                                  over(vecs[:, 2 * C:3 * C], 1, n), ALU.add).then_inc(L.v, 1)

        def rope_table(name, c, d0, d1):
            first = 0 if isinstance(c, int) and c == 0 else 1
            t = tab(name).rearrange("p (k d) -> p k d", d=D)[:, first:first + tiles_of(c), d0:d1]
            return over(t, 2, 2 * HEADS)

        def by_head(t):
            return t[:, :, :].rearrange("p j (h d) -> p j h d", d=D)

        def dve_turn(dve, L, c):
            if L.causal:
                dve.wait_ge(L.qk, 2 * c + 2)
                after(dve, L.rest, 8 * c)
                n, E2 = tiles_of(c), D // 2
                q, o = by_head(qk)[:, 0:n], by_head(yb)[:, 0:n]
                dve.tensor_tensor(o[:, :, :, 0:E2], q[:, :, :, E2:D], rope_table("sin", c, 0, E2), ALU.mult).then_inc(L.turn, 1)
                dve.tensor_tensor(o[:, :, :, E2:D], q[:, :, :, 0:E2], rope_table("sin", c, E2, D), ALU.mult).then_inc(L.turn, 1)

        def dve_squares(dve, L, c):
            if L.causal:
                dve.wait_ge(L.root, 2 * c + 1)
                n = tiles_of(c)
                dve.tensor_reduce(ss[:, 0:32 * n], yb[:, 0:n, :].rearrange("p j (h d) -> p (j h) d", d=D), AX, ALU.add).then_inc(L.turn, 1)
                dve.wait_ge(L.turn, 12 * c + 4)
                dve.tensor_scalar(msq[:, 0:32 * n], ss[:, 0:32 * n], 1.0 / D, 1e-30, ALU.mult, ALU.max).then_inc(L.turn, 1)

        def dve_scale(dve, L, c):
            if L.causal:
                k, n = 12 * c, tiles_of(c)
                dve.wait_ge(L.root, 2 * c + 2)
                dve.reciprocal(tmp[:, 0:32 * n], root0[:, 0:32 * n]).then_inc(L.turn, 1)
                dve.wait_ge(L.turn, k + 6)
                dve.tensor_tensor(tmp[:, 0:32 * n], tmp[:, 0:32 * n], msq[:, 0:32 * n], ALU.mult).then_inc(L.turn, 1)
                dve.wait_ge(L.turn, k + 7)
                dve.tensor_tensor(tmp[:, 0:32 * n], tmp[:, 0:32 * n], root0[:, 0:32 * n], ALU.add).then_inc(L.turn, 1)
                dve.wait_ge(L.turn, k + 8)
                dve.tensor_scalar(tmp[:, 0:32 * n], tmp[:, 0:32 * n], 0.5, 1e-6, ALU.mult, ALU.add).then_inc(L.turn, 1)
                dve.wait_ge(L.turn, k + 9)
                dve.reciprocal(ss[:, 0:32 * n], tmp[:, 0:32 * n]).then_inc(L.turn, 1)
                dve.wait_ge(L.turn, k + 10)
                dve.tensor_tensor(yb[:, 0:n, :].rearrange("p j (h d) -> p (j h) d", d=D),
                                  ya[:, 0:n, :].rearrange("p j (h d) -> p (j h) d", d=D),
                                  over(ss[:, 0:32 * n], 2, D), ALU.mult).then_inc(L.turn, 1)

        def dve_rest(dve, L, c, kq):
            n = tiles_of(c)
            y, st = ya if L.causal else qk, (KSt, QSt)[kq]
            dve.wait_ge(L.parts, 4 * c + kq + 1)
            if L.causal:
                dve.wait_ge(L.turn, 12 * c + 12)
            dve.tensor_tensor(heads_of(yb, kq)[:, 0:n], heads_of(y, kq)[:, 0:n], st[:, 0:n, :, 0, :], ALU.subtract).then_inc(L.rest, 1)

        def dve_low(dve, L, c):
            k, n = 8 * c, tiles_of(c)
            for kq, st in ((0, KSt), (1, QSt)):
                dve.wait_ge(L.parts, 4 * c + 2 + kq + 1)
                dve.wait_ge(L.rest, k + kq + 1)
                dve.tensor_tensor(st[:, 0:n, :, 5 if kq == 0 else 2, :], heads_of(yb, kq)[:, 0:n],
                                  st[:, 0:n, :, 3 if kq == 0 else 1, :], ALU.subtract).then_inc(L.rest, 1)
            dve.tensor_copy(KSt[:, 0:n, :, 1:3, :].rearrange("p j h a d -> p (j h) a d"),
                            over(KSt[:, 0:n, :, 0, :].rearrange("p j h d -> p (j h) d"), 2, 2)).then_inc(L.rest, 1)
            dve.tensor_copy(KSt[:, 0:n, :, 4, :], KSt[:, 0:n, :, 3, :]).then_inc(L.rest, 1)
            dve.tensor_copy(QSt[:, 0:n, :, 3:5, :], QSt[:, 0:n, :, 0:2, :]).then_inc(L.rest, 1)
            dve.tensor_copy(QSt[:, 0:n, :, 5, :], QSt[:, 0:n, :, 0, :]).then_inc(L.rest, 1)

        def dve_stacks(dve, L, c, buf, steps=range(4)):
            for s in steps:
                j, h0 = s // 2, 8 * (s % 2)
                dve.wait_ge(L.qt_ps, 4 * c + s + 1)
                if s == 0:
                    after(dve, L.st_ps, HEADS * (c - 2))
                    if isinstance(c, int) and c == 2:
                        dve.wait_ge(L.cls, 2)
                dve.tensor_copy(QT[buf][:, h0:h0 + 8, 1 + j * P:1 + (j + 1) * P],
                                bank6[:, :].bitcast(BF16)[0:KS, :].rearrange("p (h q) -> p h q", q=P)).then_inc(L.qt, stack_steps(c, s))

        def dve_max(dve, L, c, h):
            dve.wait_ge(L.sq_ps, 32 * (c - 1) + 2 * h + 2)
            if L.causal:
                for j in range(2):
                    dve.tensor_reduce(NM[:, j, h:h + 1], score_ps(L, h, j), AX, ALU.max, negate=True).then_inc(L.mx, 1)
            else:
                dve.tensor_reduce(NM[:, :, h:h + 1], bank(5 + h % 2)[:, :].rearrange("p (j q) -> p j q", j=2),
                                  AX, ALU.max, negate=True).then_inc(L.mx, 2)

        def dve_maxima(dve, L, c):
            dve.wait_ge(L.mx, 32 * c)
            after(dve, L.m3_ps, c - 1)
            if not L.causal:
                dve.wait_ge(L.ck_ps, c)
                dve.scalar_tensor_tensor(NM[:, :, :], bank7[:, 0:2 * HEADS].rearrange("p (j h) -> p j h", j=2), -1.0,
                                         NM[:, :, :], ALU.mult, ALU.min).then_inc(L.ck, 1)
                dve.wait_ge(L.ck, c)
            ms = [MS[:, :, k, 0:HEADS] for k in range(3)]
            dve.tensor_copy(ms[0], NM[:, :, :]).then_inc(L.ms, 1)
            dve.wait_ge(L.ms, 4 * (c - 1) + 1)
            dve.tensor_tensor(NR[:, :, :], NM[:, :, :], ms[0], ALU.subtract).then_inc(L.ms, 1)
            dve.wait_ge(L.ms, 4 * (c - 1) + 2)
            dve.tensor_copy(ms[1], NR[:, :, :]).then_inc(L.ms, 1)
            dve.wait_ge(L.ms, 4 * (c - 1) + 3)
            dve.tensor_tensor(ms[2], NR[:, :, :], ms[1], ALU.subtract).then_inc(L.ms, 1)

        def dve_class_maxima(dve, L, c, buf):
            n = 1 if L.causal else T
            dve.wait_ge(L.scq_ps, c)
            after(dve, L.st_ps, HEADS * (c - 2))
            k = 6 * (c - 1)
            dve.tensor_reduce(NMC[:, :], bank5[0:HEADS, 0:n], AX, ALU.max, negate=True).then_inc(L.mc, 1)
            dve.wait_ge(L.mc, k + 1)
            dve.tensor_copy(M3[buf][0:HEADS, 0:1], NMC[:, :]).then_inc(L.mc, 1)
            dve.wait_ge(L.mc, k + 2)
            dve.tensor_tensor(NRC[:, :], NMC[:, :], M3[buf][0:HEADS, 0:1], ALU.subtract).then_inc(L.mc, 1)
            dve.wait_ge(L.mc, k + 3)
            dve.tensor_copy(MC[:, :], NRC[:, :]).then_inc(L.mc, 1)
            dve.wait_ge(L.mc, k + 4)
            dve.tensor_copy(M3[buf][32:32 + HEADS, 0:1], MC[:, :]).then_inc(L.mc, 1)
            dve.tensor_tensor(M3[buf][64:64 + HEADS, 0:1], NRC[:, :], MC[:, :], ALU.subtract).then_inc(L.mc, 1)

        def dve_out(dve, L, c, j, parts=P):
            n = 4 * (c - 1) + 2 * j
            dve.wait_ge(L.to_ps, 2 * (c - 1) + j + 1)
            after(dve, L.on, n)
            after(dve, L.onT_ps, c - 1)
            v = bank7[0:parts, :].rearrange("p (h d) -> p h d", d=32)
            dve.reciprocal(RZ[0:parts, :], v[:, :, D]).then_inc(L.on, 1)
            dve.wait_ge(L.on, n + 1)
            dve.tensor_tensor(ON[0:parts, j, :].rearrange("p (h d) -> p h d", d=D), v[:, :, 0:D],
                              over(RZ[0:parts, :], 2, D), ALU.mult).then_inc(L.on, 1)

        def dve_add(dve, L, c):
            o = C if L.causal else 0
            dve.wait_ge(L.pj_ps, c)
            t = rows[:, col(2 * c, 2), o:o + C]
            dve.tensor_tensor(t, t, bank7[:, :].rearrange("p (j f) -> p j f", j=2), ALU.add).then_inc(L.h, 1)

        def dve_second(dve, L, n):
            if not L.causal:
                c = 0 if isinstance(n, int) and n == B else n + 1
                dve.wait_ge(r_res, 2 * n + 1)
                dve_norm_stats(dve, n, lambda j: tile_n(c, j), stat3, mv3, r_stat, r_mv)

        def dve_second_out(dve, L, n):
            if not L.causal:
                c = 0 if isinstance(n, int) and n == B else n + 1
                dve.wait_ge(r_res, 2 * n + 2)
                dve_norm_out(dve, n, lambda j: tile_n(c, j), lambda j: tile_n(c, j), mv3, rstd3, r_rstd, r_hn)

        def dve_clear(dve):
            dve.memset(MS[:, :, :, :], 0.0).then_inc(cleared, 1)
            dve.memset(VC[:, :, :], 0.0).then_inc(cleared, 1)
            for n in range(2):
                dve.memset(M3[n][:, :], 0.0).then_inc(cleared, 1)
                dve.memset(VA[n][:, :, :, :], 0.0).then_inc(cleared, 1)
            dve.memset(VB[:, :, :], 0.0).then_inc(cleared, 1)
            dve.memset(QZ[:, :, :], 0.0).then_inc(cleared, 1)
            dve.memset(KZ[:, :, :], 0.0).then_inc(cleared, 1)
            dve.wait_ge(cleared, 10)
            for n in range(2):
                dve.memset(VA[n][:, :, :, D:D + 1], 1.0).then_inc(cleared, 1)
            dve.tensor_copy(VB[:, :, D:D + 1], tab("own").rearrange("p (h d) -> p h d", d=D)[:, :, 0:1]).then_inc(cleared, 1)
            dve.wait_ge(cleared, 13)

        def dve_fronts(dve, L):
            for c in range(2):
                if c == 1 and L.causal:
                    dve_clear(dve)
                    dve_turn(dve, L, 0)
                    dve.wait_ge(x_loaded, 32)
                dve_stats(dve, L, c)
                dve_norm_ahead(dve, L, c, 0)
                dve_norm_ahead(dve, L, c, 1)
                dve_norm(dve, L, c)
            dve_keys_queries(dve, L, 0, 0)
            dve_v(dve, L, 0)
            dve_squares(dve, L, 0)
            dve_scale(dve, L, 0)
            for kq in range(2):
                dve_rest(dve, L, 0, kq)
            dve_low(dve, L, 0)
            dve_turn(dve, L, 1)
            dve_stacks(dve, L, 0, 0, range(2))
            dve_keys_queries(dve, L, 1, 0)
            dve_keys_queries(dve, L, 1, 1)
            dve_v(dve, L, 1)
            dve_squares(dve, L, 1)
            dve_scale(dve, L, 1)
            for kq in range(2):
                dve_rest(dve, L, 1, kq)
            dve_low(dve, L, 1)

        def dve_round(dve, L, k, buf, value=True, score=True, front=True, back=True):
            if front:
                dve_stats(dve, L, k + 2)
            for h in range(HEADS):
                if front and h == L.s_norm:
                    dve_norm(dve, L, k + 2)
                if score and h < 4:
                    dve_stacks(dve, L, k + 1, 1 - buf, [h])
                if front and h in (1, 2):
                    dve_norm_ahead(dve, L, k + 2, h - 1)
                if score:
                    for hh in score_heads(h):
                        dve_max(dve, L, k + 1, hh)
                if front:
                    if h in (L.s_front + 1, L.s_front + 2):
                        dve_keys_queries(dve, L, k + 2, h - L.s_front - 1)
                    if h == L.s_front + 3:
                        dve_v(dve, L, k + 2)
                        dve_turn(dve, L, k + 2)
                if back and h in (L.s_out, L.s_out + 1):
                    dve_out(dve, L, k - 1, h - L.s_out)
                if L.causal and front and h == L.s_square + 1:
                    dve_squares(dve, L, k + 2)
                if L.causal and front and h == L.s_square + 3:
                    dve_scale(dve, L, k + 2)
                if back and h == L.s_out + 5:
                    dve_add(dve, L, k - 1)
                if back and h == 9:
                    dve_second(dve, L, k - 2)
                if back and h == 12:
                    dve_second_out(dve, L, k - 2)
                if score and h == 13:
                    dve_maxima(dve, L, k + 1)
                if score and h == 14:
                    dve_class_maxima(dve, L, k + 1, 1 - buf)
                if front and h in (L.s_high + 1, L.s_high + 2):
                    dve_rest(dve, L, k + 2, h - L.s_high - 1)
                if front and h == 15:
                    dve_low(dve, L, k + 2)

        def dve_attention(dve, L):
            dve.wait_ge(L.in_vec, 16)
            if not L.causal:
                dve.wait_ge(L.in_w, 16)
                dve.tensor_scalar(wqkv[:, :, C:2 * C], wqkv[:, :, C:2 * C], D ** -0.5, None, ALU.mult).then_inc(cleared, 1)
            dve.tensor_scalar(vecs[:, C:2 * C], vecs[:, C:2 * C], D ** -0.5, None, ALU.mult).then_inc(cleared, 1)
            if not L.causal:
                dve.wait_ge(cleared, 15)
            dve_fronts(dve, L)
            rounds(dve, L, dve_round)
            dve_out(dve, L, B + 1, 0, parts=B)
            dve.wait_ge(L.pj_ps, B + 1)
            o = C if L.causal else 0
            dve.tensor_tensor(rows[0:B, 0, o:o + C], rows[0:B, 0, o:o + C], bank7[0:B, 0:C], ALU.add).then_inc(L.h, 1)
            dve.wait_ge(L.h, B + 1)
            dve_second(dve, L, B)
            dve_second_out(dve, L, B)

        def dve_routing(dve):
            with dve.Fori(0, TILES // 2 // GP) as m:
                for n in range(GP):
                    dve.wait_ge(r_lg_ps, GP * m + n + 1)
                    dve.tensor_tensor(lg[:, bass.ds(2 * (GP * m + n), 2), :], psT[:, n, 0:2 * E].rearrange("p (j e) -> p j e", e=E),
                                      over(lnv[:, 3 * C:3 * C + E], 1, 2), ALU.add).then_inc(r_lg, 1)
            n_r = [0]

            def step(ins):
                ins.then_inc(r_step, 1)
                n_r[0] += 1
                dve.wait_ge(r_step, n_r[0])

            dve.wait_ge(r_lg, TILES // 2)
            step(dve.tensor_reduce(lmax[:, :], lg[:, :, :], AX, ALU.max))
            step(dve.tensor_tensor(lc[:, :, :], lg[:, :, :], over(lmax[:, :], 2, E), ALU.is_equal))
            step(dve.tensor_tensor(lc[:, :, :], lc[:, :, :], tab("prefer").rearrange("p (t e) -> p t e", e=E), ALU.mult))
            step(dve.tensor_reduce(lmax[:, :], lc[:, :, :], AX, ALU.max))
            step(dve.tensor_scalar(lmax[:, :], lmax[:, :], 1.0, None, ALU.max))
            step(dve.tensor_tensor(oh[:, :, :], lc[:, :, :], over(lmax[:, :], 2, E), ALU.is_equal))
            step(dve.tensor_tensor(oh[:, :, :], oh[:, :, :], over(tab("valid"), 2, E), ALU.mult))
            dve.wait_ge(r_cnt_ps, 1)
            step(dve.tensor_copy(tot[:, :, :], bank6[:, 0:TILES * E].rearrange("p (t e) -> p e t", e=E)))
            flat = lambda t: t[:, :, :].rearrange("p e t -> p (e t)")
            step(dve.tensor_tensor_scan(flat(cum), tab("restart"), flat(tot), 0.0, ALU.mult, ALU.add))
            bigv = big[:, :].rearrange("p (e k) -> p e k", e=E)
            step(dve.tensor_tensor(bigv, over(cum[:, :, TILES - 1], 2, TILES - 1),
                                   tab("full").rearrange("p (e k) -> p e k", e=E), ALU.is_gt))
            step(dve.tensor_reduce(nt[:, :], bigv, AX, ALU.add))
            step(dve.tensor_tensor_scan(ct[:, :], tab("ones")[:, 0:E], nt[:, :], 0.0, ALU.mult, ALU.add))
            step(dve.tensor_tensor(base[:, :], ct[:, :], nt[:, :], ALU.subtract))
            step(dve.tensor_scalar(base[:, :], base[:, :], float(P), None, ALU.mult))
            step(dve.tensor_tensor(tot[:, :, :], cum[:, :, :], tot[:, :, :], ALU.subtract))
            step(dve.tensor_tensor(tot[:, :, :], tot[:, :, :], over(base[:, :], 2, TILES), ALU.add))
            step(dve.tensor_tensor(lc[:, :, :], bank5[:, 0:TILES * E].rearrange("p (t e) -> p t e", e=E),
                                   tot[:, :, :].rearrange("p e t -> p t e"), ALU.add))
            step(dve.tensor_tensor(lc[:, :, :], lc[:, :, :], oh[:, :, :], ALU.mult))
            step(dve.tensor_reduce(slotf[:, :], lc[:, :, :], AX, ALU.add))
            dve.tensor_copy(slot[:, :], slotf[:, :]).then_inc(r_slot, 1)
            step(dve.tensor_tensor(exf[:, :, :], over(ct[:, :], 1, SLOT_TILES),
                                   tab("tile_no").rearrange("p (s e) -> p s e", e=E), ALU.is_le))
            step(dve.tensor_reduce(exr[:, :], exf[:, :, :], AX, ALU.add))
            dve.tensor_scalar(ex[:, :], exr[:, :], float(E - 1), None, ALU.min).then_inc(r_ex, 1)
            dve.wait_ge(r_ex, 1)

        def dve_result(dve, s, n):
            e = expert_of(dve, s)
            dve.wait_ge(m_y_ps, s + 1)
            dve.tensor_tensor(yo[n], bank(4 + 3 * (n % 2))[:, 0:C], b2r[:, bass.ds(e, 1), :].rearrange("p o f -> p (o f)"),
                              ALU.add).then_inc(m_yb, 1)
            dve.wait_ge(m_yb, s + 1)
            dve.tensor_tensor(yo[n], yo[n], xst[n][:, C:2 * C], ALU.add).then_inc(m_yo, 1)

        def dve_expert_tile(dve, m, n):
            s = XB * m + n
            e = expert_of(dve, s)
            after(dve, m_y_ps, s - 1)
            for k in range(FC):
                if k % 4 == 0:
                    dve.wait_ge(m_midT_ps, 2 * s + k // 4 + 1)
                dve.tensor_scalar(midT[n % 2][:, k // 4, k % 4, :], psT[:, 2 * (n % 2) + k // 4, (k % 4) * P:(k % 4 + 1) * P],
                                  b1t[:, bass.ds(e, 1), k], 0.0, ALU.add, ALU.max).then_inc(m_midT, 1)
            if not (isinstance(s, int) and s == 0):
                dve_result(dve, s - 1, (n - 1) % XB)

        def dve_experts(dve):
            dve.wait_ge(in_moe, 32)
            expert_tiles(dve, dve_expert_tile)
            dve_result(dve, SLOT_TILES - 1, XB - 1)

        def root(pool, c, ve, mv, half, rstd, s_mv, s_rstd, eps):
            pool.wait_ge(s_mv, 2 * c + 2)
            settle(pool)
            pool.tensor_scalar(ve[:, :, :], mv[:, :, 1:2], eps, None, ALU.add).then_inc(s_rstd, 1)
            pool.wait_ge(s_rstd, 2 * c + 1)
            pool.tensor_tensor(rstd[:, :, :], ve[:, :, :], half.unsqueeze(2), ALU.pow).then_inc(s_rstd, 1)

        def pool_norm(pool, L, c):
            if not L.causal:
                root(pool, c, ve2, mv2, half[:, :], rstd2, L.mv_a, L.rstd_a, 1e-5)
            root(pool, c, ve, mv, half[:, :], rstd, L.mv, L.rstd, 1e-5)
            if not L.causal:
                pool.wait_ge(L.hn, 2 * c + 2)
                settle(pool)
                pool.tensor_tensor(hn[:, :, :], hn[:, :, :], over(vecs[:, 3 * C:4 * C], 1, 2), ALU.mult).then_inc(L.hb, 1)
                pool.wait_ge(L.hb, 2 * c + 1)
                settle(pool)
                pool.tensor_tensor(hn[:, :, :], hn[:, :, :], over(vecs[:, 4 * C:5 * C], 1, 2), ALU.add).then_inc(L.hb, 1)

        def pool_turn(pool, L, c):
            n = tiles_of(c)
            if L.causal:
                pool.wait_ge(L.qk, 2 * c + 2)
                after(pool, L.rest, 8 * c)
                after(pool, L.parts, 4 * c)
                pool.tensor_tensor(by_head(ya)[:, 0:n], by_head(qk)[:, 0:n], rope_table("cos", c, 0, D), ALU.mult).then_inc(L.rc, 1)
                pool.wait_ge(L.turn, 12 * c + 2)
                pool.wait_ge(L.rc, c + 1)
                settle(pool)
                pool.tensor_tensor(ya[:, 0:n, :], ya[:, 0:n, :], yb[:, 0:n, :], ALU.add).then_inc(L.turn, 1)

        def pool_weights(pool, L, c):
            if L.causal:
                pool.wait_ge(L.turn, 12 * c + 11)
                settle(pool)
                pool.tensor_tensor(ya[:, 0:tiles_of(c), :], yb[:, 0:tiles_of(c), :], over(vecs[:, 0:2 * C], 1, tiles_of(c)), ALU.mult).then_inc(L.turn, 1)

        def pool_values(pool, L, c, buf):
            pool.wait_ge(L.v, c + 1)
            after(pool, L.pv, GROUPS * (c - 2))
            settle(pool)
            pool.tensor_copy(VA[buf][:, 0:tiles_of(c), :, 0:D], by_head(vt)[:, 0:tiles_of(c)]).then_inc(L.va, 1)

        def pool_column(pool, L, c, buf):
            after(pool, L.st_ps, HEADS * (c - 2))
            after(pool, L.scq_ps, c - 1)
            settle(pool)
            pool.tensor_copy(KT[buf][:, :, 0:1], KTc[:, :, col(c - 1)]).then_inc(L.col0, 1)
            pool.tensor_copy(QT[buf][:, :, 0:1], QTc[:, :, col(c - 1)]).then_inc(L.col0, 1)
            pool.tensor_copy(QZ[:, :, HEADS - 1:HEADS], QTc[:, :, col(c - 1)]).then_inc(L.col0, 1)

        def pool_second(pool, L, n):
            if not L.causal:
                c = 0 if isinstance(n, int) and n == B else n + 1
                pool.wait_ge(L.h, n + 1)
                settle(pool)
                n2, x2 = rows[:, col(2 * c, 2), 0:C], rows[:, col(2 * c, 2), C:2 * C]
                pool.tensor_tensor(n2, n2, over(lnv[:, 2 * C:3 * C], 1, 2), ALU.add).then_inc(r_res, 1)
                pool.wait_ge(r_res, 2 * n + 1)
                settle(pool)
                pool.tensor_tensor(x2, x2, n2, ALU.add).then_inc(r_res, 1)
                root(pool, n, ve3, mv3, half[:, :], rstd3, r_mv, r_rstd, 1e-5)
                pool.wait_ge(r_hn, 2 * n + 2)
                settle(pool)
                pool.tensor_tensor(n2, n2, over(lnv[:, 0:C], 1, 2), ALU.mult).then_inc(r_hb, 1)
                pool.wait_ge(r_hb, 2 * n + 1)
                settle(pool)
                pool.tensor_tensor(n2, n2, over(lnv[:, C:2 * C], 1, 2), ALU.add).then_inc(r_hb, 1)

        def pool_class_key(pool, L, c):
            after(pool, L.sck_ps, c - 1)
            settle(pool)
            pool.tensor_copy(KZ[:, :, 3:4], KTc[:, :, col(c - 1)]).then_inc(L.vb, 1)

        def pool_class_value(pool, L, c):
            after(pool, L.pv, GROUPS * (c - 1))
            settle(pool)
            pool.tensor_tensor(VB[:, :, 0:D], over(VC[:, col(c - 1), :].rearrange("p o d -> p (o d)"), 1, HEADS),
                               tab("own").rearrange("p (h d) -> p h d", d=D), ALU.mult).then_inc(L.vb, 1)

        def pool_round(pool, L, k, buf, value=True, score=True, front=True, back=True):
            if value:
                pool_class_value(pool, L, k)
            if back:
                pool.wait_ge(L.ot_raw, GROUPS * (k - 1))
                settle(pool)
                pool.tensor_copy(OTc[:, :, col(k - 2)], OT[:, :, 0:1]).then_inc(L.otc, 1)
            if score:
                pool_column(pool, L, k + 1, 1 - buf)
                pool_class_key(pool, L, k + 1)
            if front:
                pool_norm(pool, L, k + 2)
                pool_turn(pool, L, k + 2)
                pool_weights(pool, L, k + 2)
            if back:
                pool_second(pool, L, k - 2)
            if front:
                pool_values(pool, L, k + 2, buf)

        def pool_attention(pool, L):
            pool.wait_ge(L.in_vec, 16)
            if not L.causal:
                pool.wait_ge(cleared, 15)
            pool.wait_ge(in_ln, 32)
            if L.causal:
                pool.memset(half[:, :], -0.5).then_inc(h_one, 1)
                pool.wait_ge(h_one, 5)
            pool_norm(pool, L, 0)
            pool_turn(pool, L, 0)
            pool_norm(pool, L, 1)
            pool.wait_ge(cleared, 13)
            pool_values(pool, L, 0, 0)
            pool_weights(pool, L, 0)
            pool_turn(pool, L, 1)
            pool.wait_ge(L.kt, 4)
            pool.wait_ge(L.qt, 4)
            pool.tensor_copy(KTc[:, :, :], KT[0][:, :, 1:1 + B]).then_inc(L.cls, 1)
            pool.tensor_copy(QTc[:, :, :], QT[0][:, :, 1:1 + B]).then_inc(L.cls, 1)
            pool.wait_ge(L.cls, 2)
            pool_weights(pool, L, 1)
            pool_values(pool, L, 1, 1)
            pool.wait_ge(L.vc, 64)
            rounds(pool, L, pool_round)
            pool_second(pool, L, B)

        def pool_scatter(pool):
            pool.wait_ge(r_slot, 1)
            pool.wait_ge(r_res, TILES)
            pool.wait_ge(in_cls, 32)
            pool.wait_ge(pad_stored, 16 * SLOT_TILES)
            for t in range(TILES):
                if t != 1:
                    n = B if t == 0 else P
                    pool.indirect_dma_start(out=x_sorted, out_offset=bass.IndirectOffsetOnAxis(ap=slot[0:n, t:t + 1], axis=0),
                                            in_=rows[0:n, t, :], in_offset=None).then_inc(sorted_out, 16)
            with pool.Fori(0, SLOT_TILES // XB) as m:
                for n in range(XB):
                    pool.wait_ge(m_yo, XB * m + n + 1)
                    settle(pool)
                    pool.indirect_dma_start(
                        out=out.rearrange("b t f -> (b t) f"),
                        out_offset=bass.IndirectOffsetOnAxis(ap=xst[n].bitcast(U32)[:, 2 * C:ROW], axis=0),
                        in_=yo[n], in_offset=None, bounds_check=B * T - 1, oob_is_err=False,
                    ).then_inc(m_out[n], 16)
            for n in range(XB):
                pool.wait_ge(m_out[n], 16 * (SLOT_TILES // XB))

        @block.tensor
        def _(pe):
            pe.wait_ge(in_tab, 16)
            for q in range(CH):
                pe.wait_ge(z_done, q + 1)
                pe.wait_ge(zi_done, q + 1)
                for n in range(2):
                    ps = bank5 if n == 0 else bank6
                    if q:
                        pe.wait_ge(x_sb, 2 * (q - 1) + n + 1)
                    v = ps[:, :].rearrange("p (g b) -> p g b", b=AB)
                    lo, hi = n * 64, n * 64 + 64
                    for g in range(8):
                        for part, (gg, hh) in enumerate(((gre, hre), (gim, him))):
                            for j in range(4):
                                r = 8 * j + g
                                mm = pe.matmul(v[32 * j:32 * j + 32, g, :],
                                               gg[q % 2][lo:hi, r, :, :].rearrange("p a c -> p (a c)"),
                                               hh[q % 2][lo:hi, r, :], start=(part == 0), stop=(part == 1),
                                               skip_group_check=True)
                    mm.then_inc(x_ps, 1)
            for L in layers:
                pe_attention(pe, L)
            pe_routing(pe)
            pe_experts(pe)

        @block.scalar
        def _(act):
            for q in range(CH):
                for n in range(2):
                    act.wait_ge(x_ps, 2 * q + n + 1)
                    act.activation(xs_sb[:, n, q, :, :].rearrange("p g b -> p (g b)"),
                                   (bank5 if n == 0 else bank6)[:, :], ACT.Copy).then_inc(x_sb, 1)
            store_rows(act, 1)
            load_rows(act, 1)
            for L in layers:
                act_attention(act, L)
            act.wait_ge(r_hb, TILES)
            with act.Fori(0, TILES // 2 // GP) as m:
                for n in range(GP):
                    act.activation(gn[n][:, :, :], rows[:, bass.ds(2 * (GP * m + n), 2), 0:C], ACT.Copy).then_inc(r_gn, 1)
                for n in range(GP):
                    act.wait_ge(r_gT_ps, GP * m + n + 1)
                    act.activation(gT[n][:, :, :].rearrange("p k q -> p (k q)"), bank(5 + n)[:, :], ACT.Copy).then_inc(r_gT, 1)
            act.wait_ge(r_ex, 1)
            act.wait_ge(in_w1, 32 * E)
            act.wait_ge(sorted_out, 16 * (TILES - 1))
            expert_tiles(act, act_expert_tile)

        @block.vector
        def _(dve):
            dve.memset(rows[:, 0:2, 0:2 * C], 0.0).then_inc(filled, 1)
            n_z = [0]

            def z(ins):
                ins.then_inc(z_step, 1)
                n_z[0] += 1
                dve.wait_ge(z_step, n_z[0])

            dve.wait_ge(in_z, 32)
            ex_r, ex_n, ex_p = zt[:, 0:2, :], zt[:, 2:4, :], zt[:, 4:6, :]
            ex_i = zt[:, 6:8, :].bitcast(I32)
            z(dve.tensor_scalar(ex_r, zin[:, 0:2, :], EXP_MIN, EXP_MAX, ALU.max, ALU.min))
            z(dve.tensor_scalar(ex_n, ex_r, 1 / float(np.log(2)), ROUND, ALU.mult, ALU.add))
            z(dve.tensor_scalar(ex_n, ex_n, ROUND, None, ALU.subtract))
            z(dve.scalar_tensor_tensor(ex_r, ex_n, -LN2_HIGH, ex_r, ALU.mult, ALU.add))
            dve.tensor_scalar(ex_i, ex_n, 127.0, None, ALU.add).then_inc(z_step, 1)
            n_z[0] += 1
            z(dve.scalar_tensor_tensor(ex_r, ex_n, -LN2_LOW, ex_r, ALU.mult, ALU.add))
            z(dve.tensor_scalar(ex_p, ex_r, 1 / 5040, None, ALU.mult))
            for n in (720, 120, 24, 6, 2, 1):
                z(dve.scalar_tensor_tensor(ex_p, ex_p, 1 / n, ex_r, ALU.add, ALU.mult))
            z(dve.tensor_scalar(ex_i, ex_i, 23, None, ALU.logical_shift_left))
            z(dve.scalar_tensor_tensor(ex_r, ex_p, 1.0, zt[:, 6:8, :], ALU.add, ALU.mult))
            dt, ea = zt[:, 0, :], zt[:, 1, :]
            ur, ui, den, num = (zt[:, k, :] for k in (2, 3, 4, 5))
            a, b = zt[:, 6, :], zt[:, 7, :]
            zr, zi = zp[:, 0, 0, :], zp[:, 1, 0, :]
            z(dve.scalar_tensor_tensor(ur, dt, -0.5, ea, ALU.mult, ALU.mult))
            z(dve.scalar_tensor_tensor(ui, dt, 0.5, zin[:, 2, :], ALU.mult, ALU.mult))
            z(dve.tensor_tensor(a, ur, ur, ALU.mult))
            z(dve.tensor_tensor(b, ui, ui, ALU.mult))
            z(dve.tensor_tensor(a, a, b, ALU.add))
            z(dve.tensor_scalar(num, a, -1.0, 1.0, ALU.mult, ALU.add))
            z(dve.tensor_scalar(den, ur, -1.0, 1.0, ALU.mult, ALU.add))
            z(dve.tensor_tensor(den, den, den, ALU.mult))
            z(dve.tensor_tensor(den, den, b, ALU.add))
            z(dve.reciprocal(den, den))
            z(dve.tensor_tensor(zr, num, den, ALU.mult))
            z(dve.scalar_tensor_tensor(zi, ui, 2.0, den, ALU.mult, ALU.mult))
            for k in range(8):
                zr, zi = zp[:, 0, k, :], zp[:, 1, k, :]
                if k:
                    pr, pi = zp[:, 0, k - 1, :], zp[:, 1, k - 1, :]
                    z(dve.tensor_tensor(a, pr, pr, ALU.mult))
                    z(dve.tensor_tensor(b, pi, pi, ALU.mult))
                    z(dve.tensor_tensor(zr, a, b, ALU.subtract))
                    z(dve.scalar_tensor_tensor(zi, pr, 2.0, pi, ALU.mult, ALU.mult))
                if k < 6:
                    z(dve.tensor_scalar(zn[:, k, :], zi, -1.0, None, ALU.mult))
            for n in range(2):
                dve.memset(hre[n][:, :, 0:1], 1.0).then_inc(h_one, 1)
            z(dve.tensor_scalar(zin[:, 3:5, :], zin[:, 3:5, :], 2.0, None, ALU.mult))
            n_d = 0
            for q in range(CH):
                for kind, width, k in tok_steps():
                    n = n_d + 1
                    if n > 2:
                        dve.wait_ge(pool_step, 2 * (n - 2))
                    if kind == "g0" and q >= 2:
                        dve.wait_ge(x_ps, 2 * (q - 1))
                    (xr, xi), (yr, yi), (o_r, o_i), shape = tok_operands(q, kind, width, k)
                    u1, u2, u3 = (shape(t) for t in (t1, t2, t3[n % 2]))
                    dve.tensor_tensor(u3, xr, yi, ALU.mult).then_inc(dve_step, 1)
                    dve.tensor_tensor(u1, xr, yr, ALU.mult).then_inc(z_step, 1)
                    if n > 1:
                        dve.wait_ge(pool_step, 2 * (n - 1))
                    dve.tensor_tensor(u2, xi, yi, ALU.mult).then_inc(z_step, 1)
                    n_z[0] += 2
                    dve.wait_ge(z_step, n_z[0])
                    if kind == "h" and width == 32:
                        dve.tensor_tensor(o_r, u1, u2, ALU.subtract).then_inc(z_done, 1)
                        dve.wait_ge(z_done, q + 1)
                    else:
                        z(dve.tensor_tensor(o_r, u1, u2, ALU.subtract))
                    n_d = n
            dve.wait_ge(x_ps, 2 * CH)
            dve.wait_ge(pad_stored, 16 * SLOT_TILES)
            dve.wait_ge(in_cls, 32)
            for L in layers:
                dve_attention(dve, L)
            dve_routing(dve)
            dve_experts(dve)

        @block.gpsimd
        def _(pool):
            pool.memset(pad[:, 0:2 * C], 0.0).then_inc(filled, 1)
            pool.memset(rows_i[:, 2, 2 * C:ROW], NO_ROW).then_inc(filled, 1)
            for n in range(2):
                pool.memset(him[n][:, :, 0:1], 0.0).then_inc(h_one, 1)
            pool.wait_ge(h_one, 4)
            n = 0
            for q in range(CH):
                for kind, width, k in tok_steps():
                    n += 1
                    (xr, xi), (yr, yi), (o_r, o_i), shape = tok_operands(q, kind, width, k)
                    u3, u4 = shape(t3[n % 2]), shape(t4)
                    if n > 1:
                        pool.wait_ge(pool_step, 2 * (n - 1))
                    else:
                        pool.wait_ge(dve_step, 1)
                    if kind == "g0" and q >= 2:
                        pool.wait_ge(x_ps, 2 * (q - 1))
                    pool.tensor_tensor(u4, xi, yr, ALU.mult).then_inc(pool_step, 1)
                    pool.wait_ge(pool_step, 2 * n - 1)
                    pool.wait_ge(dve_step, n)
                    pool.tensor_tensor(o_i, u3, u4, ALU.add).then_inc(pool_step, 1)
                pool.wait_ge(pool_step, 2 * n)
                pool.sem_inc(zi_done, 1)
            for L in layers:
                pool_attention(pool, L)
            pool_scatter(pool)



def kernel(**inputs):
    import concourse.bacc as _bacc
    import ml_dtypes
    from concourse.bass_utils import run_bass_kernel_spmd as _run

    a = {k: np.ascontiguousarray(v) for k, v in inputs.items()}

    def by_state(x):
        return x.reshape(2, P, NS).transpose(0, 2, 1).reshape(P, P)

    def rep(x):
        return np.broadcast_to(x.reshape(1, -1), (P, x.size))

    table, at, tableb, atb, out_row = constants()
    log_dt = np.broadcast_to(a["L0_tok_log_dt"][:, None], (2 * P, NS))
    b_ri, c_ri = a["L0_tok_B_ri"], a["x"]
    f = lambda k: a["L0_ffn_" + k]
    ker = dict(
        table=table, tableb=tableb.astype(ml_dtypes.bfloat16), out_row=out_row,
        z_in=np.stack([by_state(x) for x in (log_dt, a["L0_tok_inv_A_real"], a["L0_tok_A_imag"], b_ri[..., 0], b_ri[..., 1])], 1),
        c_in=np.stack([np.stack([by_state(c_ri[b, :, :, k]) for b in range(B)], 1) for k in range(2)], 1),
        cls=np.broadcast_to(a["cls_tok"].reshape(1, C), (B, C)),
        wqkv=np.stack([a["L0_attn_W_kqv"].T, np.concatenate([f("wk"), f("wq"), f("wv")], 1)]),
        wout=np.stack([a["L0_attn_W_proj"].T, f("wo")]),
        vecs=np.stack([
            np.concatenate([rep(np.tile(a["L0_attn_k_norm_w"], HEADS)), rep(np.tile(a["L0_attn_q_norm_w"], HEADS)),
                            np.zeros((P, 3 * C), np.float32)], 1),
            np.concatenate([rep(f(k)) for k in ("bk", "bq", "bv", "ln1_g", "ln1_b")], 1)]),
        lnv=np.concatenate([rep(f(k)) for k in ("ln2_g", "ln2_b", "bo", "gate_b")], 1),
        gate_w=f("gate_w"), w1=f("w1"), w2=f("w2"),
        b1t=f("b1").reshape(E, FC, P).transpose(2, 0, 1),
        b2r=np.broadcast_to(f("b2")[None], (P, E, C)),
    )
    nc = _bacc.Bacc("TRN2", target_bir_lowering=False, num_devices=1)
    arrays, args = {}, {}
    for k, v in ker.items():
        arrays["in_" + k] = np.ascontiguousarray(v)
        args[k] = nc.dram_tensor("in_" + k, v.shape, mybir.dt.from_np(v.dtype), kind="ExternalInput").ap()
    out = nc.dram_tensor("out", (B, T, C), F32, kind="ExternalOutput").ap()
    bass_vit_tower(nc, args, out, at, atb, table.shape[1], tableb.shape[1])
    r = _run(nc, [arrays], core_ids=[0])
    return r.results[0]["out"]
```
